# Optimizing a Trainium2 kernel written in Bass

```python
import numpy as np
import jax
import jax.numpy as jnp

def _softmax(x, axis=-1):
    return jax.nn.softmax(x, axis=axis)

def _gelu(x):
    return jax.nn.gelu(x, approximate=True)

def _silu(x):
    return jax.nn.silu(x)

def _sigmoid(x):
    return jax.nn.sigmoid(x)

def _layernorm(x, axis=-1, eps=1e-05):
    m = jnp.mean(x, axis=axis, keepdims=True)
    v = jnp.var(x, axis=axis, keepdims=True)
    return (x - m) / jnp.sqrt(v + eps)

def _scatter_add(tgt, idx, src, axis=0):
    return tgt.at[idx].add(src)

def _segment_sum(src, seg, n):
    return jax.ops.segment_sum(src, seg, n)
kernel_name = 'mk_seq_preln_d1_jaxref_r4_9e2440'

def setup_inputs(seed: int=0):
    np.random.seed(seed)
    _w = jnp.asarray

    def _L0_attn_setup():
        import jax, jax.numpy as jnp
        import numpy as np
        B, T, D = (2, 512, 512)
        QH, KVH = (16, 4)
        HD = D // QH

        def rotate_half(x):
            d = x.shape[-1] // 2
            return jnp.concatenate([-x[..., d:], x[..., :d]], axis=-1)

        def rope_tables(head_dim, seq_len, theta=10000.0):
            freqs = 1.0 / theta ** (jnp.arange(0, head_dim, 2, dtype=jnp.float32) / head_dim)
            t = jnp.arange(seq_len, dtype=jnp.float32)
            ang = t[:, None] * freqs[None, :]
            cos = jnp.tile(jnp.cos(ang), (1, 2))
            sin = jnp.tile(jnp.sin(ang), (1, 2))
            return (cos, sin)

        def apply_rope(x, cos, sin):
            c = cos[None, None, :, :]
            s = sin[None, None, :, :]
            return x * c + rotate_half(x) * s
        key = jax.random.key(seed)
        kx, kq, kk, kv, ko = jax.random.split(key, 5)
        scale = D ** (-0.5)
        return {'x': jax.random.normal(kx, (B, T, D), dtype=jnp.float32), 'wq': jax.random.normal(kq, (D, D), dtype=jnp.float32) * scale, 'wk': jax.random.normal(kk, (D, KVH * HD), dtype=jnp.float32) * scale, 'wv': jax.random.normal(kv, (D, KVH * HD), dtype=jnp.float32) * scale, 'wo': jax.random.normal(ko, (D, D), dtype=jnp.float32) * scale}
    _L0_attn_in = _L0_attn_setup()

    def _L0_ffn_setup():
        import jax, jax.numpy as jnp
        import numpy as np
        BLOCK_SIZE = 32
        HIDDEN_SIZE = 512
        MLP_DIM = 4096
        NVFP4_LUT = jnp.array([0.0, 0.5, 1.0, 1.5, 2.0, 3.0, 4.0, 6.0, 0.0, -0.5, -1.0, -1.5, -2.0, -3.0, -4.0, -6.0], dtype=jnp.float32)

        def dequant_nvfp4(W_packed, scales, block=BLOCK_SIZE):
            N = W_packed.shape[0]
            low = W_packed & 15
            high = W_packed >> 4 & 15
            idx = jnp.stack([low, high], axis=-1).reshape(N, -1)
            vals = NVFP4_LUT[idx]
            K = vals.shape[1]
            vals = vals.reshape(N, K // block, block) * scales[:, :, None]
            return vals.reshape(N, K)
        key = jax.random.key(seed)
        ks = jax.random.split(key, 7)
        x = jax.random.normal(ks[0], (4, 32, HIDDEN_SIZE), dtype=jnp.float32)
        gate_W_packed = jax.random.randint(ks[1], (MLP_DIM, HIDDEN_SIZE // 2), 0, 64, dtype=jnp.int32)
        gate_scales = jax.random.uniform(ks[2], (MLP_DIM, HIDDEN_SIZE // BLOCK_SIZE), dtype=jnp.float32) * 0.1 + 0.001
        up_W_packed = jax.random.randint(ks[3], (MLP_DIM, HIDDEN_SIZE // 2), 0, 64, dtype=jnp.int32)
        up_scales = jax.random.uniform(ks[4], (MLP_DIM, HIDDEN_SIZE // BLOCK_SIZE), dtype=jnp.float32) * 0.1 + 0.001
        down_W_packed = jax.random.randint(ks[5], (HIDDEN_SIZE, MLP_DIM // 2), 0, 64, dtype=jnp.int32)
        down_scales = jax.random.uniform(ks[6], (HIDDEN_SIZE, MLP_DIM // BLOCK_SIZE), dtype=jnp.float32) * 0.1 + 0.001
        return {'x': x, 'gate_W_packed': gate_W_packed, 'gate_scales': gate_scales, 'up_W_packed': up_W_packed, 'up_scales': up_scales, 'down_W_packed': down_W_packed, 'down_scales': down_scales}
    _L0_ffn_in = _L0_ffn_setup()
    _d = {'L0_attn_x': _L0_attn_in['x'], 'L0_attn_wq': _L0_attn_in['wq'], 'L0_attn_wk': _L0_attn_in['wk'], 'L0_attn_wv': _L0_attn_in['wv'], 'L0_attn_wo': _L0_attn_in['wo'], 'L0_ffn_gate_W_packed': _L0_ffn_in['gate_W_packed'], 'L0_ffn_gate_scales': _L0_ffn_in['gate_scales'], 'L0_ffn_up_W_packed': _L0_ffn_in['up_W_packed'], 'L0_ffn_up_scales': _L0_ffn_in['up_scales'], 'L0_ffn_down_W_packed': _L0_ffn_in['down_W_packed'], 'L0_ffn_down_scales': _L0_ffn_in['down_scales']}
    _x0 = _d['L0_attn_x']
    _d['L0_attn_x'] = jax.random.normal(jax.random.fold_in(jax.random.key(seed), 1), (2, 1024, 512), dtype=_x0.dtype)
    del _x0
    return _d

def reference(L0_attn_x, L0_attn_wq, L0_attn_wk, L0_attn_wv, L0_attn_wo, L0_ffn_gate_W_packed, L0_ffn_gate_scales, L0_ffn_up_W_packed, L0_ffn_up_scales, L0_ffn_down_W_packed, L0_ffn_down_scales):

    def _L0_attn_ref(x, wq, wk, wv, wo):
        import jax, jax.numpy as jnp
        import numpy as np
        B, T, D = (2, 512, 512)
        QH, KVH = (16, 4)
        HD = D // QH

        def rotate_half(x):
            d = x.shape[-1] // 2
            return jnp.concatenate([-x[..., d:], x[..., :d]], axis=-1)

        def rope_tables(head_dim, seq_len, theta=10000.0):
            freqs = 1.0 / theta ** (jnp.arange(0, head_dim, 2, dtype=jnp.float32) / head_dim)
            t = jnp.arange(seq_len, dtype=jnp.float32)
            ang = t[:, None] * freqs[None, :]
            cos = jnp.tile(jnp.cos(ang), (1, 2))
            sin = jnp.tile(jnp.sin(ang), (1, 2))
            return (cos, sin)

        def apply_rope(x, cos, sin):
            c = cos[None, None, :, :]
            s = sin[None, None, :, :]
            return x * c + rotate_half(x) * s
        b, t, d = x.shape
        cos, sin = rope_tables(HD, t)
        q = (x @ wq).reshape(b, t, QH, HD).transpose(0, 2, 1, 3)
        k = (x @ wk).reshape(b, t, KVH, HD).transpose(0, 2, 1, 3)
        v = (x @ wv).reshape(b, t, KVH, HD).transpose(0, 2, 1, 3)
        q = apply_rope(q, cos, sin)
        k = apply_rope(k, cos, sin)
        g = QH // KVH
        k = jnp.repeat(k, g, axis=1)
        v = jnp.repeat(v, g, axis=1)
        attn = jnp.einsum('bhqd,bhkd->bhqk', q, k) / np.sqrt(HD)
        mask = jnp.triu(jnp.ones((t, t), dtype=bool), k=1)
        attn = jnp.where(mask[None, None], -jnp.inf, attn)
        attn = jax.nn.softmax(attn, axis=-1)
        out = jnp.einsum('bhqk,bhkd->bhqd', attn, v)
        out = out.transpose(0, 2, 1, 3).reshape(b, t, d)
        return out @ wo

    def _L0_ffn_ref(x, gate_W_packed, gate_scales, up_W_packed, up_scales, down_W_packed, down_scales):
        import jax, jax.numpy as jnp
        import numpy as np
        BLOCK_SIZE = 32
        HIDDEN_SIZE = 512
        MLP_DIM = 4096
        NVFP4_LUT = jnp.array([0.0, 0.5, 1.0, 1.5, 2.0, 3.0, 4.0, 6.0, 0.0, -0.5, -1.0, -1.5, -2.0, -3.0, -4.0, -6.0], dtype=jnp.float32)

        def dequant_nvfp4(W_packed, scales, block=BLOCK_SIZE):
            N = W_packed.shape[0]
            low = W_packed & 15
            high = W_packed >> 4 & 15
            idx = jnp.stack([low, high], axis=-1).reshape(N, -1)
            vals = NVFP4_LUT[idx]
            K = vals.shape[1]
            vals = vals.reshape(N, K // block, block) * scales[:, :, None]
            return vals.reshape(N, K)
        B, S, H = x.shape
        xt = x.reshape(B * S, H)
        Wg = dequant_nvfp4(gate_W_packed, gate_scales)
        Wu = dequant_nvfp4(up_W_packed, up_scales)
        Wd = dequant_nvfp4(down_W_packed, down_scales)
        gate = jnp.einsum('th,nh->tn', xt, Wg)
        up = jnp.einsum('th,nh->tn', xt, Wu)
        gelu = jnp.tanh(0.7978845608028654 * (gate + 0.044715 * gate ** 3)) * gate * 0.5 + gate * 0.5
        inter = gelu * up
        out = jnp.einsum('tn,hn->th', inter, Wd)
        return out.reshape(B, S, H)
    x = L0_attn_x
    x = x + _L0_attn_ref(_layernorm(x, axis=-1), L0_attn_wq, L0_attn_wk, L0_attn_wv, L0_attn_wo)
    x = x + _L0_ffn_ref(_layernorm(x, axis=-1), L0_ffn_gate_W_packed, L0_ffn_gate_scales, L0_ffn_up_W_packed, L0_ffn_up_scales, L0_ffn_down_W_packed, L0_ffn_down_scales)
    return x

_drawn_inputs = setup_inputs


def setup_inputs(seed=0):
    import zlib

    import numpy as np

    out = dict(_drawn_inputs(seed))
    spreads = {}
    factors = {}
    for name, (base, spread) in spreads.items():
        noise = np.random.default_rng([zlib.crc32(name.encode()), seed]).standard_normal(out[name].shape)
        drawn = base * np.exp(spread * noise) if base else spread * noise
        out[name] = jnp.asarray(drawn.astype(out[name].dtype))
    for name, factor in factors.items():
        out[name] = (out[name] * factor).astype(out[name].dtype)
    return out
```

```python
from contextlib import ExitStack

import concourse.bass as bass
import numpy as np
from concourse import mybir

F32 = mybir.dt.float32
F32R = mybir.dt.float32r
BF16 = mybir.dt.bfloat16
FP8 = mybir.dt.float8e5
I32 = mybir.dt.int32
U32 = mybir.dt.uint32
ALU = mybir.AluOpType
ACT = mybir.ActivationFunctionType
AX_X = mybir.AxisListType.X

P = 128
B, T, D = 2, 1024, 512
HEADS, KV_HEADS, HD = 16, 4, 32
REP = HEADS // KV_HEADS
KV = KV_HEADS * HD
MLP, QBLOCK = 4096, 32
TILES = B * T // P
QT_TILES = T // P
DC = D // P
BANK = 512
EPS = 1e-5
MASKED = -1e30
VW = 2 * HD + 1
GELU_C, GELU_A = 0.7978845608028654, 0.044715

GROUP = 2 * P
GROUPS = MLP // GROUP
CHUNKS = B * T // BANK
WORDS = D // 2 * GROUP // P
CODE_SCALE = float(2 ** 14)


class Slots:

    def __init__(self, count, period, first, lag):
        self.count, self.period, self.first, self.lag = count, period, first, lag

    def run(self, eng, emit):
        loops = (self.count - self.first) // self.period
        for j in range(self.first):
            emit(0, j)
        with eng.Fori(0, loops) as k:
            for j in range(self.first, self.first + self.period):
                emit(k, j)
        for j in range(self.first, self.count + self.lag - loops * self.period):
            emit(loops, j)

    def live(self, k, j):
        return not isinstance(k, int) or 0 <= self.period * k + j < self.count


def wait(eng, sem, value):
    if not isinstance(value, int) or value > 0:
        eng.wait_ge(sem, value)


def block_kernel(nc, x_in, wq_in, wk_in, wv_in, wo_in, rope_in, codes_in, scales_in, out):
    with ExitStack() as ctx:
        def sem(name):
            return ctx.enter_context(nc.semaphore(name))

        def in_scope(scope):
            return lambda name, cols, dt=F32: scope.enter_context(nc.sbuf_tensor(name, [P, cols], dt))

        sb = in_scope(ctx)
        x_res = sb("x_res", TILES * D)
        ident = sb("ident", P)
        ident_bf = sb("ident_bf", P, BF16)
        causal = sb("causal", P, BF16)
        causal_t = sb("causal_t", BANK, BF16)
        stats = sb("stats", 2 * 6)
        mean_var = sb("mean_var", 4 * 2)
        var_eps = sb("var_eps", 4)
        rstd = sb("rstd", 4)
        minus_half = sb("minus_half", 1)
        xn = [sb(f"xn{r}", D) for r in range(2)]
        lhs_hi = [sb(f"lhs_hi{r}", D, F32R) for r in range(2)]
        lhs_lo = [sb(f"lhs_lo{r}", D, F32R) for r in range(2)]
        neg_part = [sb(f"neg_part{r}", REP * 2) for r in range(2)]
        neg_max = sb("neg_max", REP)
        max_parts = [sb(f"max_parts{r}", REP * 2, F32R) for r in range(2)]
        inv_sum = [sb(f"inv_sum{r}", REP) for r in range(2)]

        with ExitStack() as scope_c:
            sb = in_scope(scope_c)
            q_nat = sb("q_nat", KV_HEADS * TILES * P)
            wo_hi = sb("wo_hi", DC * D, F32R)
            wo_lo = sb("wo_lo", DC * D, F32R)
            attn = [sb(f"attn{r}", D) for r in range(2)]
            with ExitStack() as scope_ab:
                sb = in_scope(scope_ab)
                v_nat = sb("v_nat", KV_HEADS * TILES * HD)
                k_stack = sb("k_stack", KV_HEADS * TILES * P, F32R)
                with ExitStack() as scope_a:
                    sb = in_scope(scope_a)
                    W = D + 2 * KV
                    w_raw = sb("w_raw", DC * W)
                    w_hi = sb("w_hi", DC * W, F32R)
                    w_lo = sb("w_lo", DC * W, F32R)
                    rope = sb("rope", TILES * 4 * HD)
                    qk_raw = [sb(f"qk_raw{r}", D + KV) for r in range(2)]
                    by_cos = [sb(f"by_cos{r}", D + KV) for r in range(2)]
                    by_sin = [sb(f"by_sin{r}", D + KV) for r in range(2)]
                    k_nat = [sb(f"k_nat{r}", KV) for r in range(2)]
                    k_parts = [sb(f"k_parts{r}", 4 * KV, F32R) for r in range(2)]
                sb = in_scope(scope_ab)
                wo_raw = sb("wo_raw", DC * D)
                k_blocks = sb("k_blocks", T, F32R)
                v_blocks = sb("v_blocks", QT_TILES * VW, F32R)
                probs = [sb(f"probs{r}", BANK) for r in range(4)]
                probs_hi = [sb(f"probs_hi{r}", BANK, F32R) for r in range(4)]
                probs_lo = [sb(f"probs_lo{r}", BANK, F32R) for r in range(4)]
                out_t = [sb(f"out_t{r}", BANK) for r in range(2)]
                part_hi = [sb(f"part_hi{r}", P) for r in range(2)]
                part_lo = [sb(f"part_lo{r}", P) for r in range(2)]
                q_parts = [sb(f"q_parts{r}", REP * 4 * HD, F32R) for r in range(2)]
                q_stack = [sb(f"q_stack{r}", REP * P, F32R) for r in range(4)]
            with ExitStack() as scope_d:
                sb = in_scope(scope_d)
                xt_hi = sb("xt_hi", DC * B * T, F32R)
                xt_lo = sb("xt_lo", DC * B * T, F32R)
                wg_hi, wg_lo = [None, None], [None, None]
                wg_hi[0] = sb("wg_hi0", 6 * WORDS, F32R)
                wg_lo[0] = sb("wg_lo0", 6 * WORDS, F32R)
                codes = sb("codes", 3 * WORDS, I32)
                scales = sb("scales", 3 * WORDS)
                bits_a = sb("bits_a", WORDS, U32)
                bits_b = sb("bits_b", WORDS, U32)
                w_full = sb("w_full", 2 * WORDS)
        sb = in_scope(ctx)
        wg_hi[1] = sb("wg_hi1", 6 * WORDS, F32R)
        wg_lo[1] = sb("wg_lo1", 6 * WORDS, F32R)
        act_hi = [sb(f"act_hi{r}", BANK, F32R) for r in range(4)]
        act_lo = [sb(f"act_lo{r}", BANK, F32R) for r in range(4)]
        y_buf = [sb(f"y_buf{r}", BANK) for r in range(2)]

        psum = ctx.enter_context(nc.psum_tensor("psum", [P, 8 * BANK], F32))

        def bank(n, cols=BANK, at=0):
            return psum[:, n * BANK + at:n * BANK + at + cols]

        x_in_dma = [sem("x_in_dma0"), sem("x_in_dma1")]
        w_dma, rope_dma, wo_dma = sem("w_dma"), sem("rope_dma"), sem("wo_dma")
        consts = sem("consts")
        w_hi_done, w_lo_done = sem("w_hi_done"), sem("w_lo_done")
        wo_hi_done, wo_lo_done = sem("wo_hi_done"), sem("wo_lo_done")
        a_stats, a_mean, a_veps, a_rstd, a_xn = (sem("a_" + n) for n in ("stats", "mean", "veps", "rstd", "xn"))
        a_xt_ps, a_xt_hi, a_xt_lo = sem("a_xt_ps"), sem("a_xt_hi"), sem("a_xt_lo")
        a_qkv_ps, a_qkv_sb, a_rope, a_rotated, a_k_hi, a_k_parts, a_kt_ps, a_kt_sb = (sem("a_" + n) for n in (
            "qkv_ps", "qkv_sb", "rope", "rotated", "k_hi", "k_parts", "kt_ps", "kt_sb"))
        b_q_hi, b_q_parts, b_qt_ps, b_qt_sb = sem("b_q_hi"), sem("b_q_parts"), sem("b_qt_ps"), sem("b_qt_sb")
        b_by_query, b_part_max, b_max, b_max_hi, b_max_parts, b_mt_ps, b_mt_sb = (sem("b_" + n) for n in (
            "by_query", "part_max", "max", "max_hi", "max_parts", "mt_ps", "mt_sb"))
        b_by_key, b_exp, b_pv = sem("b_by_key"), sem("b_exp"), sem("b_pv")
        b_hi = [sem("b_hi_even"), sem("b_hi_odd")]
        b_lo = [sem("b_lo_even"), sem("b_lo_odd")]
        b_k_block, b_v_hi, b_v_block = sem("b_k_block"), sem("b_v_hi"), sem("b_v_block")
        b_out_sb, b_out_ps, b_inv, b_scaled, b_out = (sem("b_" + n) for n in (
            "out_sb", "out_ps", "inv", "scaled", "out"))
        c_attn, c_at_ps, c_at_hi, c_at_lo, c_proj, c_x, c_stats, c_mean, c_veps, c_rstd, c_xn, c_xt_ps, c_xt_hi, \
            c_xt_lo = (sem("c_" + n) for n in ("attn", "at_ps", "at_hi", "at_lo", "proj", "x", "stats", "mean",
                                               "veps", "rstd", "xn", "xt_ps", "xt_hi", "xt_lo"))
        codes_dma, scales_dma = sem("codes_dma"), sem("scales_dma")
        d_bits, d_w, d_w_hi, d_w_lo = sem("d_bits"), sem("d_w"), sem("d_w_hi"), sem("d_w_lo")
        d_gate, d_up, d_square, d_inner, d_tanh, d_gelu, d_y, d_y_hi, d_y_lo, d_down, d_acc = (
            sem("d_" + n) for n in ("gate", "up", "square", "inner", "tanh", "gelu", "y", "y_hi", "y_lo", "down",
                                    "acc"))
        out_dma = sem("out_dma")
        waits_of_pool, waits_of_dve = sem("waits_of_pool"), sem("waits_of_dve")

        passed = {}

        def wait_apart(eng, sem, value):
            wait(eng, sem, value)
            if not isinstance(value, int):
                eng.sem_inc(passed[eng.engine])

        def f32(ap):
            return ap.bitcast(F32)

        def by_g(ap, cols):
            return ap.rearrange("p (g c) -> p g c", g=KV_HEADS, c=cols)

        A = Slots(TILES, period=4, first=6, lag=4)

        def x_tile(t):
            return x_res[:, bass.ds(t * D, D)]

        PAIR_CHUNKS = QT_TILES * (QT_TILES + 1) // 2
        UNITS = KV_HEADS * B * QT_TILES
        BS = Slots(KV_HEADS * B * PAIR_CHUNKS, period=PAIR_CHUNKS, first=10, lag=7)
        FIRST_CHUNK = [i * (i + 1) // 2 for i in range(QT_TILES + 1)]

        def chunk(k, j):
            c = j % PAIR_CHUNKS
            i = max(i for i in range(QT_TILES) if FIRST_CHUNK[i] <= c)
            pair = k + j // PAIR_CHUNKS
            return pair, i, c - FIRST_CHUNK[i], QT_TILES * pair + i, PAIR_CHUNKS * k + j

        def unit_ahead(pair, i, ahead):
            pair, i = pair + (i + ahead) // QT_TILES, (i + ahead) % QT_TILES
            u = QT_TILES * pair + i
            return None if isinstance(u, int) and u >= UNITS else (pair, i, u)

        def n_parts(i):
            return -(-(i + 1) * P // BANK)

        PARTS_BEFORE = [REP * sum(n_parts(a) for a in range(i)) for i in range(QT_TILES + 1)]

        def parts(pair, i):
            at = [(h, c) for h in range(REP) for c in range(n_parts(i))]
            return [(PARTS_BEFORE[-1] * pair + PARTS_BEFORE[i] + n, n % 2, h, c, c * BANK,
                     min((i + 1) * P - c * BANK, BANK)) for n, (h, c) in enumerate(at)]

        def parts_ahead(pair, i, kb):
            if not (unit := unit_ahead(pair, i, 2)):
                return None, []
            p = parts(*unit[:2])
            return unit, p[len(p) * kb // (i + 1):len(p) * (kb + 1) // (i + 1)]

        C = Slots(TILES, period=2, first=6, lag=4)

        GROUP_ITEMS = CHUNKS * 2
        DS = Slots(GROUPS * GROUP_ITEMS, period=2 * GROUP_ITEMS, first=GROUP_ITEMS, lag=2)
        PIECE_AT = {2: 0, 4: 1, 6: 2}

        def piece(k, j):
            if j % GROUP_ITEMS in PIECE_AT and DS.live(k, j + GROUP_ITEMS):
                m = PIECE_AT[j % GROUP_ITEMS]
                g = j // GROUP_ITEMS + 1
                return m, g % 2, 6 * k + 3 * g + m
            return None

        def columns(buf, m):
            return buf[:, m * 2 * WORDS:(m + 1) * 2 * WORDS]

        CONSTS_A = 13

        def half_count(k, j):
            return PAIR_CHUNKS // 2 * k + j // 2 + 1

        block = ctx.enter_context(nc.Block())

        @block.sync
        def _(sp):
            for u in range(TILES // 2):
                wait(sp, x_in_dma[u % 2], 16 * (u // 2))
                sp.dma_start(x_res[:, u * 2 * D:(u + 1) * 2 * D].rearrange("p (n d) -> p n d", n=2),
                             x_in[u * 2 * P:(u + 1) * 2 * P, :].rearrange("(n p) d -> p n d", p=P)
                             ).then_inc(x_in_dma[u % 2], 16)
            sp.wait_ge(a_kt_sb, TILES)
            sp.wait_ge(a_k_parts, TILES)
            sp.dma_start(wo_raw[:].rearrange("p (c n) -> p c n", c=DC),
                         wo_in.rearrange("(c p) n -> p c n", p=P)).then_inc(wo_dma, 16)
            sp.wait_ge(b_out, KV_HEADS * TILES)
            sp.wait_ge(wo_lo_done, 1)

            def load_group(g):
                sp.dma_start(codes[:], codes_in[bass.ds(g, 1), :, :].rearrange("g p w -> (g p) w")
                             ).then_inc(codes_dma, 16)
                sp.dma_start(scales[:], scales_in[bass.ds(g, 1), :, :].rearrange("g s w -> (g s) w").unsqueeze(1)
                             .broadcast_to([P // 16, 16, 3 * WORDS])).then_inc(scales_dma, 16)

            load_group(0)
            with sp.Fori(1, GROUPS) as g:
                sp.wait_ge(d_w, g * 3)
                load_group(g)
            for j in range(CHUNKS):
                sp.wait_ge(d_acc, 4 * ((GROUPS - 1) * CHUNKS + j + 1))
                sp.dma_start(out[j * BANK:(j + 1) * BANK, :].rearrange("(n p) d -> p n d", p=P),
                             x_res[:, j * 4 * D:(j + 1) * 4 * D].rearrange("p (n d) -> p n d", n=4)
                             ).then_inc(out_dma, 16)
            sp.wait_ge(out_dma, 16 * CHUNKS)

        @block.gpsimd
        def _(pool):
            passed[pool.engine] = waits_of_pool
            pool.memset(minus_half[:], -0.5).then_inc(consts, 1)
            pool.memset(ident[:], 0.0).then_inc(consts, 1)
            pool.memset(ident_bf[:], 0.0).then_inc(consts, 1)
            pool.memset(causal[:], 0.0).then_inc(consts, 1)
            pool.memset(causal_t[:], 0.0).then_inc(consts, 1)
            for r in range(2):
                first = by_g(k_parts[r][:], P)[:, :, 0:HD]
                pool.memset(f32(first), 0.0).then_inc(consts, 1)
            pool.wait_ge(consts, 7)
            for r in range(2):
                pool.memset(f32(by_g(k_parts[r][:], P)[:, :, 0:2]), 1.0).then_inc(consts, 1)
            for m in (ident, ident_bf):
                pool.affine_select(out=m[:], in_=m[:], compare_op=ALU.not_equal, fill=1.0, base=0,
                                   pattern=[[-1, P]], channel_multiplier=1).then_inc(consts, 1)
            pool.affine_select(out=causal[:], in_=causal[:], compare_op=ALU.is_ge, fill=MASKED, base=0,
                               pattern=[[-1, P]], channel_multiplier=1).then_inc(consts, 1)
            causal_t3 = causal_t[:].rearrange("p (h q) -> p h q", h=REP)
            pool.affine_select(out=causal_t3, in_=causal_t3, compare_op=ALU.is_ge, fill=MASKED, base=0,
                               pattern=[[0, REP], [1, P]], channel_multiplier=-1).then_inc(consts, 1)

            def inverse_deviation(t, r, mean_sem, veps_sem, rstd_sem):
                wait_apart(pool, mean_sem, t + 1)
                pool.tensor_scalar(var_eps[:, r:r + 1], mean_var[:, 2 * r + 1:2 * r + 2], EPS, None,
                                   ALU.add).then_inc(veps_sem, 1)
                pool.wait_ge(veps_sem, t + 1)
                pool.tensor_tensor(rstd[:, r:r + 1], var_eps[:, r:r + 1], minus_half[:],
                                   ALU.pow).then_inc(rstd_sem, 1)

            def slot_a(k, j):
                t, r = A.period * k + j, j % 4
                if A.live(k, j):
                    inverse_deviation(t, r, a_mean, a_veps, a_rstd)
                if A.live(k, j - 3):
                    t, r = t - 3, (j - 3) % 2
                    wait_apart(pool, a_rope, t + 1)
                    wait_apart(pool, a_k_parts, t - 1)
                    cos, sin = (s[r][:].rearrange("p (h a d) -> p h a d", a=2, d=HD // 2) for s in (by_cos, by_sin))
                    q_out = q_nat[:].rearrange("p (g c) -> p g c", g=KV_HEADS)[:, :, bass.ds(t * P, P)]
                    k_out = k_nat[r][:].rearrange("p (h a d) -> p h a d", a=2, d=HD // 2)
                    for a in range(2):
                        pool.tensor_tensor(
                            q_out.rearrange("p g (h a d) -> p g h a d", a=2, d=HD // 2)[:, :, :, a, :],
                            cos[:, 0:HEADS, a, :].rearrange("p (g h) d -> p g h d", g=KV_HEADS),
                            sin[:, 0:HEADS, 1 - a, :].rearrange("p (g h) d -> p g h d", g=KV_HEADS), ALU.add)
                        rot = pool.tensor_tensor(k_out[:, :, a, :], cos[:, HEADS:, a, :], sin[:, HEADS:, 1 - a, :],
                                                 ALU.add)
                    rot.then_inc(a_rotated, 1)
                    wait_apart(pool, a_rotated, t + 1)
                    wait_apart(pool, a_kt_ps, t - 1)
                    slots = k_parts[r][:].rearrange("p (g s d) -> p g s d", g=KV_HEADS, s=4)
                    k_in = k_nat[r][:].rearrange("p (g d) -> p g d", d=HD)
                    twice = k_nat[r][:].rearrange("p (g d) -> p g d", d=HD).unsqueeze(2).broadcast_to(
                        [P, KV_HEADS, 2, HD])
                    pool.tensor_copy(slots[:, :, 1:3, :], twice).then_inc(a_k_hi, 1)
                    pool.wait_ge(a_k_hi, t + 1)
                    pool.tensor_tensor(slots[:, :, 3, :], k_in, f32(slots[:, :, 1, :]),
                                       ALU.subtract).then_inc(a_k_parts, 1)

            A.run(pool, slot_a)

            pool.wait_ge(a_kt_sb, TILES)
            for r in range(2):
                pool.memset(f32(q_parts[r][:].rearrange("p (h c) -> p h c", h=REP)[:, :, 0:HD]), 0.0).then_inc(consts, 1)
            v_ones = v_blocks[:].rearrange("p (b c) -> p b c", b=QT_TILES)[:, :, VW - 1:VW]
            pool.memset(f32(v_ones), 1.0).then_inc(consts, 1)
            pool.wait_ge(consts, CONSTS_A + 3)

            def query_parts(pair, i, u):
                wait_apart(pool, b_qt_ps, u - 1)
                slots = q_parts[i % 2][:].rearrange("p (h s d) -> p h s d", h=REP, s=4)
                q_in = q_nat[:, bass.ds(u * P, P)].rearrange("p (h d) -> p h d", h=REP)
                pool.tensor_copy(slots[:, :, 1::2, :], q_in.unsqueeze(2).broadcast_to([P, REP, 2, HD])
                                 ).then_inc(b_q_hi, 1)
                wait_apart(pool, b_q_hi, u + 1)
                pool.tensor_tensor(slots[:, :, 2, :], q_in, f32(slots[:, :, 1, :]),
                                   ALU.subtract).then_inc(b_q_parts, 1)

            def pair_block(pair, kb):
                n = QT_TILES * pair + kb
                pool.tensor_copy(k_blocks[:, kb * P:(kb + 1) * P], k_stack[:, bass.ds(pair * T + kb * P, P)]
                                 ).then_inc(b_k_block, 1)
                v_in = v_nat[:, bass.ds(pair * QT_TILES * HD + kb * HD, HD)]
                v_hi = v_blocks[:, kb * VW:kb * VW + HD]
                pool.tensor_copy(v_hi, v_in).then_inc(b_v_hi, 1)
                wait_apart(pool, b_v_hi, n + 1)
                pool.tensor_tensor(v_blocks[:, kb * VW + HD:kb * VW + 2 * HD], v_in, f32(v_hi),
                                   ALU.subtract).then_inc(b_v_block, 1)

            for i in range(2):
                query_parts(0, i, i)
            for kb in range(QT_TILES):
                pair_block(0, kb)
            for i in range(2, 4):
                query_parts(0, i, i)

            def slot_b(k, j):
                if BS.live(k, j):
                    pair, i, kb, u, n = chunk(k, j)
                    if kb == 0 and (unit := unit_ahead(pair, i, 4)):
                        query_parts(*unit)
                if BS.live(k, j - 1) and j % 2 == 1:
                    r = (j - 1) % 4
                    n = PAIR_CHUNKS * k + j - 1
                    pool.wait_ge(b_hi[0], half_count(k, j - 1))
                    pool.tensor_tensor(probs_lo[r][:], probs[r][:], f32(probs_hi[r][:]),
                                       ALU.subtract).then_inc(b_lo[0], 1)
                if BS.live(k, j - 4):
                    pair, i, kb, u, n = chunk(k, j - 4)
                    if i == QT_TILES - 1 and unit_ahead(pair, i, 1):
                        wait_apart(pool, b_pv, n + 1)
                        pair_block(pair + 1, kb)
                if BS.live(k, j - 7):
                    pair, i, kb, u, n = chunk(k, j - 7)
                    if kb == i:
                        wait_apart(pool, b_scaled, u + 1)
                        pool.tensor_tensor(q_nat[:, bass.ds(u * P, P)], part_hi[i % 2][:], part_lo[i % 2][:],
                                           ALU.add).then_inc(b_out, 1)

            BS.run(pool, slot_b)
            pool.wait_ge(b_out, KV_HEADS * TILES)

            def weights_low(m, buf, n):
                pool.wait_ge(d_w_hi, n + 1)
                pool.tensor_tensor(columns(wg_lo[buf], m), w_full[:], f32(columns(wg_hi[buf], m)),
                                   ALU.subtract).then_inc(d_w_lo, 1)

            for m in range(3):
                weights_low(m, 0, m)

            def slot_c(k, j):
                t = 2 * k + j
                if C.live(k, j):
                    wait_apart(pool, c_at_ps, t - 1)
                    pool.tensor_copy(by_g(attn[j % 2][:], P),
                                     q_nat[:].rearrange("p (g c) -> p g c", g=KV_HEADS)[:, :, bass.ds(t * P, P)]
                                     ).then_inc(c_attn, 1)
                if C.live(k, j - 2):
                    inverse_deviation(t - 2, j % 2, c_mean, c_veps, c_rstd)

            C.run(pool, slot_c)

            def slot_d(k, j):
                s = DS.period * k + j
                if p := piece(k, j):
                    weights_low(*p)
                if DS.live(k, j):
                    pool.wait_ge(d_y_hi, s + 1)
                    pool.tensor_tensor(act_lo[j % 4][:], y_buf[j % 2][:], f32(act_hi[j % 4][:]),
                                       ALU.subtract).then_inc(d_y_lo, 1)

            DS.run(pool, slot_d)

        @block.scalar
        def _(act):
            w3 = w_raw[:].rearrange("p (c n) -> p c n", c=DC)
            for src, at, n in ((wq_in, 0, D), (wk_in, D, KV), (wv_in, D + KV, KV)):
                act.dma_start(w3[:, :, at:at + n], src.rearrange("(c p) n -> p c n", p=P)).then_inc(w_dma, 16)
            for b in range(B):
                act.dma_start(rope[:].rearrange("p (b n c) -> p b n c", b=B, n=QT_TILES)[:, b],
                              rope_in.rearrange("(n p) c -> p n c", p=P)).then_inc(rope_dma, 16)
            act.wait_ge(w_dma, 48)
            act.activation(w_hi[:], w_raw[:], ACT.Copy).then_inc(w_hi_done, 1)

            def slot_a(k, j):
                t = A.period * k + j
                if A.live(k, j - 1):
                    r = (j - 1) % 2
                    act.wait_ge(a_xt_ps, t)
                    wait(act, a_qkv_ps, t - 2)
                    act.activation(lhs_hi[r][:], bank(r), ACT.Copy).then_inc(a_xt_hi, 1)
                if A.live(k, j - 4):
                    act.wait_ge(a_kt_ps, t - 3)
                    act.activation(by_g(k_stack[:], B * T)[:, :, bass.ds((t - 4) * P, P)],
                                   by_g(bank(6 + j % 2), P), ACT.Copy).then_inc(a_kt_sb, 1)
                if A.live(k, j - 2):
                    r = j % 2
                    act.wait_ge(a_qkv_ps, t - 1)
                    wait(act, a_rope, t - 3)
                    act.activation(by_g(v_nat[:], TILES * HD)[:, :, bass.ds((t - 2) * HD, HD)],
                                   by_g(bank(3 + 2 * r, KV, KV), HD), ACT.Copy)
                    act.activation(qk_raw[r][:], psum[:, (2 + 2 * r) * BANK:(2 + 2 * r) * BANK + D + KV],
                                   ACT.Copy).then_inc(a_qkv_sb, 1)

            A.run(act, slot_a)
            act.wait_ge(wo_dma, 16)
            act.activation(wo_hi[:], wo_raw[:], ACT.Copy).then_inc(wo_hi_done, 1)

            def queries_out(pair, i, u):
                act.wait_ge(b_qt_ps, u + 1)
                wait(act, b_by_key, PAIR_CHUNKS * (pair - (i < 4)) + FIRST_CHUNK[(i - 4) % 8 + 1])
                act.activation(q_stack[i % 4][:], bank(5), ACT.Copy).then_inc(b_qt_sb, 1)

            def maxima_out(pair, i, u):
                act.wait_ge(b_mt_ps, u + 1)
                act.activation(q_stack[i % 4][0:2, :], psum[0:2, 5 * BANK:6 * BANK], ACT.Copy).then_inc(b_mt_sb, 1)

            for i in range(3):
                queries_out(0, i, i)
            maxima_out(0, 0, 0)

            def slot_b(k, j):
                if BS.live(k, j):
                    pair, i, kb, u, n = chunk(k, j)
                    act.wait_ge(b_by_key, n + 1)
                    wait(act, b_pv, n - 3)
                    act.activation(probs[j % 4][:], bank(2 + j % 2), ACT.Exp).then_inc(b_exp, 1)
                    if kb == 0 and (unit := unit_ahead(pair, i, 1)):
                        maxima_out(*unit)
                    if j % 2 == 0:
                        act.wait_ge(b_exp, n + 1)
                        act.activation(probs_hi[j % 4][:], probs[j % 4][:], ACT.Copy).then_inc(b_hi[0], 1)
                    if kb == i and (unit := unit_ahead(pair, i, 3)):
                        queries_out(*unit)
                if BS.live(k, j - 4):
                    pair, i, kb, u, n = chunk(k, j - 4)
                    if kb == i:
                        act.wait_ge(b_pv, n + 1)
                        wait(act, b_out_ps, u - 1)
                        act.activation(out_t[i % 2][0:VW, :], bank(4 + 3 * (i % 2))[0:VW, :],
                                       ACT.Copy).then_inc(b_out_sb, 1)

            BS.run(act, slot_b)

            def weights_high(m, buf, n):
                act.wait_ge(d_w, n + 1)
                act.activation(columns(wg_hi[buf], m), w_full[:], ACT.Copy).then_inc(d_w_hi, 1)

            for m in range(3):
                weights_high(m, 0, m)

            def slot_c(k, j):
                t = 2 * k + j
                if C.live(k, j - 1):
                    r = (j - 1) % 2
                    act.wait_ge(c_at_ps, t)
                    wait(act, c_proj, t - 2)
                    act.activation(lhs_hi[r][:], bank(r), ACT.Copy).then_inc(c_at_hi, 1)
                if C.live(k, j - 4):
                    act.wait_ge(c_xt_ps, t - 3)
                    act.activation(xt_hi[:].rearrange("p (c t) -> p c t", c=DC)[:, :, bass.ds((t - 4) * P, P)],
                                   bank(4 + j % 2).rearrange("p (c t) -> p c t", c=DC),
                                   ACT.Copy).then_inc(c_xt_hi, 1)

            C.run(act, slot_c)

            def slot_d(k, j):
                s = DS.period * k + j
                if DS.live(k, j):
                    y = y_buf[j % 2]
                    act.wait_ge(d_gate, s + 1)
                    wait(act, d_y_lo, s - 1)
                    act.activation(y[:], bank(j % 2), ACT.Square).then_inc(d_square, 1)
                    act.wait_ge(d_inner, s + 1)
                    act.activation(y[:], y[:], ACT.Tanh, scale=GELU_C * GELU_A).then_inc(d_tanh, 1)
                if p := piece(k, j):
                    wait(act, d_down, DS.period * k + j // GROUP_ITEMS * GROUP_ITEMS)
                    weights_high(*p)
                if DS.live(k, j):
                    act.wait_ge(d_y, s + 1)
                    wait(act, d_down, s - 3)
                    act.activation(act_hi[j % 4][:], y[:], ACT.Copy).then_inc(d_y_hi, 1)

            DS.run(act, slot_d)

        @block.vector
        def _(dve):
            passed[dve.engine] = waits_of_dve
            def moments(t, r, r4, stats_sem, mean_sem):
                st = stats[:, 6 * r:6 * r + 6]
                dve.bn_stats(st, x_tile(t)).then_inc(stats_sem, 1)
                wait_apart(dve, stats_sem, t + 1)
                dve.bn_aggr(mean_var[:, 2 * r4:2 * r4 + 2], st).then_inc(mean_sem, 1)

            def normalise(t, r, r4, xn_sem):
                dve.tensor_scalar(xn[r][:], x_tile(t), mean_var[:, 2 * r4:2 * r4 + 1], rstd[:, r4:r4 + 1],
                                  ALU.subtract, ALU.mult).then_inc(xn_sem, 1)

            def slot_a(k, j):
                t = A.period * k + j
                if A.live(k, j):
                    wait_apart(dve, x_in_dma[j // 2 % 2], 16 * (k + j // 4 + 1))
                    moments(t, j % 2, j % 4, a_stats, a_mean)
                if j == 0 and isinstance(k, int) and k == 0:
                    dve.wait_ge(w_hi_done, 1)
                    dve.tensor_tensor(w_lo[:], w_raw[:], f32(w_hi[:]), ALU.subtract).then_inc(w_lo_done, 1)
                    dve.wait_ge(rope_dma, 32)
                if A.live(k, j - 1):
                    dve.wait_ge(a_rstd, t)
                    wait(dve, a_xt_ps, t - 2)
                    normalise(t - 1, (j - 1) % 2, (j - 1) % 4, a_xn)
                if A.live(k, j - 3):
                    r = (j - 3) % 2
                    dve.wait_ge(a_qkv_sb, t - 2)
                    wait(dve, a_rotated, t - 4)
                    for i, (at, n) in enumerate(((0, HEADS), (D, KV_HEADS))):
                        for which, dst in enumerate((by_cos[r], by_sin[r])):
                            table = rope[:, bass.ds((t - 3) * 4 * HD + (2 * i + which) * HD, HD)]
                            last = dve.tensor_tensor(
                                dst[:, at:at + n * HD].rearrange("p (h d) -> p h d", d=HD),
                                qk_raw[r][:, at:at + n * HD].rearrange("p (h d) -> p h d", d=HD),
                                table.unsqueeze(1).broadcast_to([P, n, HD]), ALU.mult)
                    last.then_inc(a_rope, 1)
                if A.live(k, j - 1):
                    r = (j - 1) % 2
                    dve.wait_ge(a_xt_hi, t)
                    dve.tensor_tensor(lhs_lo[r][:], bank(r), f32(lhs_hi[r][:]), ALU.subtract).then_inc(a_xt_lo, 1)

            A.run(dve, slot_a)
            dve.wait_ge(wo_hi_done, 1)
            dve.tensor_tensor(wo_lo[:], wo_raw[:], f32(wo_hi[:]), ALU.subtract).then_inc(wo_lo_done, 1)

            def part_maxima(pair, i, u, pieces):
                for n, r, h, c, at, keys in pieces:
                    dve.wait_ge(b_by_query, n + 1)
                    dve.tensor_reduce(neg_part[i % 2][:, 2 * h + c:2 * h + c + 1], bank(r, keys), axis=AX_X,
                                      op=ALU.max, negate=True).then_inc(b_part_max, 1)
                if pieces and pieces[-1][2] == REP - 1 and pieces[-1][3] == n_parts(i) - 1:
                    dve.wait_ge(b_part_max, pieces[-1][0] + 1)
                    each = neg_part[i % 2][:].rearrange("p (h c) -> p h c", h=REP)[:, :, 0:n_parts(i)]
                    dve.tensor_reduce(neg_max[:], each, axis=AX_X, op=ALU.min).then_inc(b_max, 1)
                    dve.wait_ge(b_max, u + 1)
                    wait(dve, b_mt_ps, u - 1)
                    both = max_parts[i % 2][:].rearrange("p (h s) -> p h s", h=REP)
                    dve.tensor_copy(both[:, :, 0], neg_max[:]).then_inc(b_max_hi, 1)
                    dve.wait_ge(b_max_hi, u + 1)
                    dve.tensor_tensor(both[:, :, 1], neg_max[:], f32(both[:, :, 0]),
                                      ALU.subtract).then_inc(b_max_parts, 1)

            for i in range(2):
                part_maxima(0, i, i, parts(0, i))

            def slot_b(k, j):
                if BS.live(k, j):
                    pair, i, kb, u, n = chunk(k, j)
                    unit, pieces = parts_ahead(pair, i, kb)
                    if unit:
                        part_maxima(*unit, pieces)
                if BS.live(k, j - 1) and j % 2 == 0:
                    r = (j - 1) % 4
                    dve.wait_ge(b_exp, PAIR_CHUNKS * k + j)
                    dve.tensor_copy(probs_hi[r][:], probs[r][:]).then_inc(b_hi[1], 1)
                    dve.wait_ge(b_hi[1], half_count(k, j - 1))
                    dve.tensor_tensor(probs_lo[r][:], probs[r][:], f32(probs_hi[r][:]),
                                      ALU.subtract).then_inc(b_lo[1], 1)
                if BS.live(k, j - 6):
                    pair, i, kb, u, n = chunk(k, j - 6)
                    if kb == i:
                        out3 = bank(6, REP * VW).rearrange("p (h c) -> p h c", h=REP)
                        inv = inv_sum[i % 2]
                        dve.wait_ge(b_out_ps, u + 1)
                        dve.reciprocal(inv[:], out3[:, :, VW - 1]).then_inc(b_inv, 1)
                        dve.wait_ge(b_inv, u + 1)
                        wait(dve, b_out, u - 1)
                        inv3 = inv[:].unsqueeze(2).broadcast_to([P, REP, HD])
                        for dst, at in ((part_hi, 0), (part_lo, HD)):
                            last = dve.tensor_tensor(dst[i % 2][:].rearrange("p (h d) -> p h d", h=REP),
                                                     out3[:, :, at:at + HD], inv3, ALU.mult)
                        last.then_inc(b_scaled, 1)

            BS.run(dve, slot_b)

            def unpack(m, n, group_count):
                if m == 0:
                    dve.wait_ge(codes_dma, group_count)
                    dve.wait_ge(scales_dma, group_count)
                words = codes[:, m * WORDS:(m + 1) * WORDS].bitcast(U32)
                dve.tensor_scalar(bits_a[:], words, 12, 0xF0000, ALU.logical_shift_left,
                                  ALU.bitwise_and).then_inc(d_bits, 1)
                dve.wait_ge(d_bits, 4 * n + 1)
                dve.scalar_tensor_tensor(bits_b[:], words, 0xF, bits_a[:], ALU.bitwise_and,
                                         ALU.bitwise_or).then_inc(d_bits, 1)
                dve.wait_ge(d_bits, 4 * n + 2)
                dve.scalar_tensor_tensor(bits_a[:], bits_b[:], 3, bits_b[:], ALU.logical_shift_left,
                                         ALU.bitwise_or).then_inc(d_bits, 1)
                dve.wait_ge(d_bits, 4 * n + 3)
                dve.tensor_scalar(bits_b[:], bits_a[:], 1, 0x008E008E, ALU.logical_shift_left,
                                  ALU.bitwise_and).then_inc(d_bits, 1)
                wait_apart(dve, d_bits, 4 * n + 4)
                wait_apart(dve, d_w_lo, n)
                value = bits_b[:].bitcast(FP8).rearrange("p (w b) -> p b w", b=4)
                for nibble in range(2):
                    last = dve.scalar_tensor_tensor(w_full[:, nibble * WORDS:(nibble + 1) * WORDS],
                                                    value[:, 2 * nibble, :], CODE_SCALE,
                                                    scales[:, m * WORDS:(m + 1) * WORDS], ALU.mult, ALU.mult)
                last.then_inc(d_w, 1)

            for m in range(3):
                unpack(m, m, 16)

            def slot_c(k, j):
                t = 2 * k + j
                if C.live(k, j - 1):
                    r = (j - 1) % 2
                    dve.wait_ge(c_at_hi, t)
                    dve.tensor_tensor(lhs_lo[r][:], bank(r), f32(lhs_hi[r][:]), ALU.subtract).then_inc(c_at_lo, 1)
                if C.live(k, j - 3):
                    dve.wait_ge(c_rstd, t - 2)
                    wait(dve, c_xt_ps, t - 4)
                    normalise(t - 3, (j - 3) % 2, (j - 3) % 2, c_xn)
                if C.live(k, j - 4):
                    dve.wait_ge(c_xt_hi, t - 3)
                    dst, hi = (b[:].rearrange("p (c t) -> p c t", c=DC)[:, :, bass.ds((t - 4) * P, P)]
                               for b in (xt_lo, xt_hi))
                    dve.tensor_tensor(dst, bank(4 + j % 2).rearrange("p (c t) -> p c t", c=DC), f32(hi),
                                      ALU.subtract).then_inc(c_xt_lo, 1)
                if C.live(k, j - 2):
                    dve.wait_ge(c_proj, t - 1)
                    dve.tensor_tensor(x_tile(t - 2), x_tile(t - 2), bank(2 + j % 2), ALU.add).then_inc(c_x, 1)
                    wait_apart(dve, c_x, t - 1)
                    moments(t - 2, j % 2, j % 2, c_stats, c_mean)

            C.run(dve, slot_c)

            def slot_d(k, j):
                s = DS.period * k + j
                y, gate, up = y_buf[j % 2], bank(j % 2), bank(2 + j % 2)
                if DS.live(k, j):
                    dve.wait_ge(d_square, s + 1)
                    dve.scalar_tensor_tensor(y[:], y[:], 1.0 / GELU_A, gate, ALU.add, ALU.mult).then_inc(d_inner, 1)
                if p := piece(k, j):
                    m, buf, n = p
                    unpack(m, n, 16 * (2 * k + j // GROUP_ITEMS + 2))
                if DS.live(k, j):
                    dve.wait_ge(d_tanh, s + 1)
                    dve.scalar_tensor_tensor(y[:], y[:], 1.0, gate, ALU.add, ALU.mult).then_inc(d_gelu, 1)
                    dve.wait_ge(d_gelu, s + 1)
                    dve.wait_ge(d_up, s + 1)
                    dve.scalar_tensor_tensor(y[:], y[:], 0.5, up, ALU.mult, ALU.mult).then_inc(d_y, 1)
                if j % 2 == 1 and DS.live(k, j - 2):
                    dve.wait_ge(d_down, s - 1)
                    for n in range(4):
                        tile = (j - 2) // 2 % CHUNKS * 4 + n
                        x = x_res[:, tile * D:(tile + 1) * D]
                        dve.tensor_tensor(x, x, bank(4 + n), ALU.add).then_inc(d_acc, 1)

            DS.run(dve, slot_d)

        @block.tensor
        def _(pe):
            pe.wait_ge(consts, CONSTS_A)
            pe.wait_ge(w_lo_done, 1)

            def split_product(dst, lhs, rhs, first=True, last=True, n=DC):
                for c in range(n):
                    for q, (a, b) in enumerate(((0, 0), (0, 1), (1, 0))):
                        mm = pe.matmul(dst, lhs(a, c), rhs(b, c), start=first and c == 0 and q == 0,
                                       stop=last and c == n - 1 and q == 2)
                return mm

            def slot_a(k, j):
                t = A.period * k + j
                if A.live(k, j - 1):
                    r = (j - 1) % 2
                    pe.wait_ge(a_xn, t)
                    wait(pe, a_xt_lo, t - 2)
                    for c in range(DC):
                        tr = pe.transpose(bank(r, P, c * P), xn[r][:, c * P:(c + 1) * P], ident[:])
                    tr.then_inc(a_xt_ps, 1)
                if A.live(k, j - 2):
                    r = j % 2
                    pe.wait_ge(a_xt_hi, t - 1)
                    pe.wait_ge(a_xt_lo, t - 1)
                    wait(pe, a_qkv_sb, t - 3)
                    for dst, at, n in ((bank(2 + 2 * r), 0, D), (bank(3 + 2 * r, 2 * KV), D, 2 * KV)):
                        mm = split_product(
                            dst, lambda a, c: (lhs_hi, lhs_lo)[a][r][:, c * P:(c + 1) * P],
                            lambda b, c: (w_hi, w_lo)[b][:, c * W + at:c * W + at + n])
                    mm.then_inc(a_qkv_ps, 1)
                if A.live(k, j - 4):
                    r = j % 2
                    pe.wait_ge(a_k_parts, t - 3)
                    wait(pe, a_kt_sb, t - 5)
                    for g in range(KV_HEADS):
                        tr = pe.transpose(bank(6 + r, P, g * P), f32(k_parts[r][:, g * P:(g + 1) * P]), ident[:])
                    tr.then_inc(a_kt_ps, 1)

            A.run(pe, slot_a)
            pe.wait_ge(a_kt_sb, TILES)

            def queries(pair, i, u):
                pe.wait_ge(b_q_parts, u + 1)
                wait(pe, b_qt_sb, u)
                wait(pe, b_mt_sb, 0 if isinstance(u, int) and u < 3 else u - 1)
                for h in range(REP):
                    tr = pe.transpose(bank(5, P, h * P), f32(q_parts[i % 2][:, h * P:(h + 1) * P]), ident[:])
                tr.then_inc(b_qt_ps, 1)

            def maxima(pair, i, u):
                pe.wait_ge(b_max_parts, u + 1)
                if isinstance(u, int):
                    pe.wait_ge(b_qt_sb, min(max(u + 2, 3), UNITS))
                else:
                    pe.wait_ge(b_qt_sb, u + 2)
                for h in range(REP):
                    tr = pe.transpose(psum[0:2, 5 * BANK + h * P:5 * BANK + (h + 1) * P],
                                      f32(max_parts[i % 2][:, 2 * h:2 * h + 2]), ident[:])
                tr.then_inc(b_mt_ps, 1)

            def scores_by_query(pair, i, u, pieces):
                for n, r, h, c, at, keys in pieces:
                    if n is pieces[0][0]:
                        pe.wait_ge(b_qt_sb, u + 1)
                    wait(pe, b_part_max, n - 1)
                    diagonal = at + keys == (i + 1) * P
                    mm = pe.matmul(bank(r, keys), q_stack[i % 4][:, h * P:(h + 1) * P],
                                   k_stack[:, bass.ds(pair * T + at, keys)], start=True, stop=not diagonal)
                    if diagonal:
                        mm = pe.matmul(bank(r, P, keys - P), ident_bf[:], causal[:], start=False, stop=True)
                    mm.then_inc(b_by_query, 1)

            for i in range(3):
                queries(0, i, i)
            for i in range(2):
                scores_by_query(0, i, i, parts(0, i))
            maxima(0, 0, 0)

            def slot_b(k, j):
                if BS.live(k, j):
                    pair, i, kb, u, n = chunk(k, j)
                    if kb == 0:
                        pe.wait_ge(b_mt_sb, u + 1)
                    if kb == i:
                        pe.wait_ge(b_k_block, QT_TILES * pair + kb + 1)
                    wait(pe, b_exp, n - 1)
                    mm = pe.matmul(bank(2 + j % 2), k_blocks[:, kb * P:(kb + 1) * P], q_stack[i % 4][:],
                                   start=True, stop=kb != i)
                    if kb == i:
                        mm = pe.matmul(bank(2 + j % 2), ident_bf[:], causal_t[:], start=False, stop=True)
                    mm.then_inc(b_by_key, 1)
                    unit, pieces = parts_ahead(pair, i, kb)
                    if unit:
                        scores_by_query(*unit, pieces)
                if BS.live(k, j - 3):
                    pair, i, kb, u, n = chunk(k, j - 3)
                    if kb == 0:
                        wait(pe, b_out_sb, u - 1)
                    if kb == i:
                        pe.wait_ge(b_v_block, QT_TILES * pair + kb + 1)
                    r = (j - 3) % 4
                    pe.wait_ge(b_lo[r % 2], half_count(k, j - 3))
                    for q, part in enumerate((probs_hi, probs_lo)):
                        mm = pe.matmul(bank(4 + 3 * (i % 2))[0:VW, :], v_blocks[:, kb * VW:(kb + 1) * VW], part[r][:],
                                       start=kb == 0 and q == 0, stop=kb == i and q == 1)
                    mm.then_inc(b_pv, 1)
                if BS.live(k, j):
                    pair, i, kb, u, n = chunk(k, j)
                    if kb == 0 and (unit := unit_ahead(pair, i, 1)):
                        maxima(*unit)
                    if kb == i and (unit := unit_ahead(pair, i, 3)):
                        queries(*unit)
                if BS.live(k, j - 5):
                    pair, i, kb, u, n = chunk(k, j - 5)
                    if kb == i:
                        pe.wait_ge(b_out_sb, u + 1)
                        wait(pe, b_scaled, u)
                        for h in range(REP):
                            tr = pe.transpose(bank(6, VW, h * VW), out_t[i % 2][0:VW, h * P:(h + 1) * P],
                                              ident[0:VW, 0:VW])
                        tr.then_inc(b_out_ps, 1)

            BS.run(pe, slot_b)
            pe.wait_ge(wo_lo_done, 1)
            pe.wait_ge(b_out, KV_HEADS * TILES)

            def slot_c(k, j):
                t = 2 * k + j
                if C.live(k, j - 1):
                    r = (j - 1) % 2
                    pe.wait_ge(c_attn, t)
                    wait(pe, c_at_lo, t - 2)
                    for c in range(DC):
                        tr = pe.transpose(bank(r, P, c * P), attn[r][:, c * P:(c + 1) * P], ident[:])
                    tr.then_inc(c_at_ps, 1)
                if C.live(k, j - 2):
                    r = j % 2
                    pe.wait_ge(c_at_hi, t - 1)
                    pe.wait_ge(c_at_lo, t - 1)
                    wait(pe, c_x, t - 3)
                    mm = split_product(bank(2 + r), lambda a, c: (lhs_hi, lhs_lo)[a][r][:, c * P:(c + 1) * P],
                                       lambda b, c: (wo_hi, wo_lo)[b][:, c * D:(c + 1) * D])
                    mm.then_inc(c_proj, 1)
                if C.live(k, j - 4):
                    r = j % 2
                    pe.wait_ge(c_xn, t - 3)
                    wait(pe, c_xt_lo, t - 5)
                    for c in range(DC):
                        half, parity = c // 2, c % 2
                        tr = pe.transpose(bank(4 + r, P, c * P),
                                          xn[r][:, half * 2 * P + parity:(half + 1) * 2 * P:2], ident[:])
                    tr.then_inc(c_xt_ps, 1)

            C.run(pe, slot_c)
            pe.wait_ge(c_xt_lo, TILES)

            def slot_d(k, j):
                s = DS.period * k + j
                if DS.live(k, j):
                    g, chunk, half = j // GROUP_ITEMS, j // 2 % CHUNKS, j % 2
                    wait(pe, d_y, s - 1)
                    for m, done in ((0, d_gate), (1, d_up)):
                        if j % GROUP_ITEMS == 0:
                            pe.wait_ge(d_w_lo, 6 * k + 3 * g + m + 1)
                        split_product(
                            bank(2 * m + j % 2),
                            lambda a, c: columns((wg_hi, wg_lo)[a][g % 2], m)[
                                :, c % 2 * WORDS + c // 2 * GROUP + half * P:
                                c % 2 * WORDS + c // 2 * GROUP + (half + 1) * P],
                            lambda b, c: (xt_hi, xt_lo)[b][:, c * B * T + chunk * BANK:
                                                           c * B * T + (chunk + 1) * BANK]).then_inc(done, 1)
                if DS.live(k, j - 2):
                    i = j - 2
                    g, half = i // GROUP_ITEMS, i % 2
                    if i % GROUP_ITEMS == 0:
                        pe.wait_ge(d_w_lo, 6 * k + 3 * g + 3)
                    pe.wait_ge(d_y_hi, s - 1)
                    pe.wait_ge(d_y_lo, s - 1)
                    for n in range(4):
                        if half == 0:
                            wait(pe, d_acc, 4 * (DS.period // 2 * k + i // 2 - 1) + n + 1)
                        mm = split_product(
                            bank(4 + n), lambda a, c: (act_hi, act_lo)[a][i % 4][:, n * P:(n + 1) * P],
                            lambda b, c: columns((wg_hi, wg_lo)[b][g % 2], 2)[:, half * WORDS:(half + 1) * WORDS],
                            first=half == 0, last=half == 1, n=1)
                    mm.then_inc(d_down, 1)

            DS.run(pe, slot_d)


def rope_tables():
    freqs = (1.0 / np.float32(10000.0) ** (np.arange(0, HD, 2, dtype=np.float32) / np.float32(HD))).astype(np.float32)
    angle = np.arange(T, dtype=np.float32)[:, None] * freqs[None, :]
    cos, sin = np.cos(angle), np.sin(angle)
    q = np.concatenate([cos, cos, sin, -sin], axis=1)
    return np.concatenate([q, q / np.float32(np.sqrt(HD))], axis=1).astype(np.float32)


def kernel(**inputs):
    import concourse.bacc as bacc
    from concourse.bass_utils import run_bass_kernel_spmd

    a = {n.split("_", 1)[1]: np.asarray(v) for n, v in inputs.items()}
    pair, blocks = P, GROUP // QBLOCK
    codes, scales = [], []
    for n in ("gate", "up"):
        w = a[f"ffn_{n}_W_packed"].reshape(GROUPS, pair, 2, 2, P)
        codes.append(w.transpose(0, 4, 3, 2, 1).reshape(GROUPS, P, WORDS))
        s = a[f"ffn_{n}_scales"].reshape(GROUPS, pair, 2, 2, blocks)
        scales.append(s.transpose(0, 4, 3, 2, 1).reshape(GROUPS, blocks, WORDS))
    codes.append(a["ffn_down_W_packed"].reshape(D, GROUPS, P).transpose(1, 2, 0))
    scales.append(a["ffn_down_scales"].reshape(D, GROUPS, blocks).transpose(1, 2, 0))
    arrays = {
        "x": a["attn_x"].reshape(B * T, D), "wq": a["attn_wq"], "wk": a["attn_wk"], "wv": a["attn_wv"],
        "wo": a["attn_wo"], "rope": rope_tables(),
        "codes": np.concatenate(codes, axis=2), "scales": np.concatenate(scales, axis=2),
    }
    arrays = {n: np.ascontiguousarray(v) for n, v in arrays.items()}
    nc = bacc.Bacc("TRN2", target_bir_lowering=False, num_devices=1)
    args = [nc.dram_tensor(f"in_{n}", v.shape, mybir.dt.from_np(v.dtype), kind="ExternalInput").ap()
            for n, v in arrays.items()]
    out = nc.dram_tensor("out", (B * T, D), F32, kind="ExternalOutput").ap()
    block_kernel(nc, *args, out)
    r = run_bass_kernel_spmd(nc, [{f"in_{n}": v for n, v in arrays.items()}], core_ids=[0])
    return r.results[0]["out"].reshape(B, T, D)
```

```python
from contextlib import ExitStack

import concourse.bass as bass
import numpy as np
from concourse import mybir

F32 = mybir.dt.float32
F32R = mybir.dt.float32r
BF16 = mybir.dt.bfloat16
FP8 = mybir.dt.float8e5
I32 = mybir.dt.int32
U32 = mybir.dt.uint32
ALU = mybir.AluOpType
ACT = mybir.ActivationFunctionType
AX_X = mybir.AxisListType.X

P = 128
B, T, D = 2, 1024, 512
HEADS, KV_HEADS, HD = 16, 4, 32
REP = HEADS // KV_HEADS
KV = KV_HEADS * HD
MLP, QBLOCK = 4096, 32
TILES = B * T // P
QT_TILES = T // P
DC = D // P
BANK = 512
EPS = 1e-5
MASKED = -1e30
VW = 2 * HD + 1
GELU_C, GELU_A = 0.7978845608028654, 0.044715

GROUP = 2 * P
GROUPS = MLP // GROUP
CHUNKS = B * T // BANK
WORDS = D // 2 * GROUP // P
CODE_SCALE = float(2 ** 14)


class Slots:

    def __init__(self, count, period, first, lag, lead=0):
        self.count, self.period, self.first, self.lag, self.lead = count, period, first, lag, lead

    def run(self, eng, emit):
        loops = (self.count - self.first) // self.period
        for j in range(-self.lead, self.first):
            emit(0, j)
        with eng.Fori(0, loops) as k:
            for j in range(self.first, self.first + self.period):
                emit(k, j)
        for j in range(self.first, self.count + self.lag - loops * self.period):
            emit(loops, j)

    def live(self, k, j):
        return not isinstance(k, int) or 0 <= self.period * k + j < self.count


def wait(eng, sem, value):
    if not isinstance(value, int) or value > 0:
        eng.wait_ge(sem, value)


def block_kernel(nc, x_in, wq_in, wk_in, wv_in, wo_in, rope_in, codes_in, scales_in, out):
    with ExitStack() as ctx:
        def sem(name):
            return ctx.enter_context(nc.semaphore(name))

        def in_scope(scope):
            return lambda name, cols, dt=F32: scope.enter_context(nc.sbuf_tensor(name, [P, cols], dt))

        sb = in_scope(ctx)
        x_res = sb("x_res", TILES * D)
        ident = sb("ident", P)
        ident_r = sb("ident_r", P, F32R)
        ident_bf = sb("ident_bf", P, BF16)
        causal = sb("causal", P, BF16)
        causal_t = sb("causal_t", BANK, BF16)
        stats = sb("stats", 2 * 6)
        mean_var = sb("mean_var", 4 * 2)
        var_eps = sb("var_eps", 4)
        rstd = sb("rstd", 4)
        minus_half = sb("minus_half", 1)
        xn = [sb(f"xn{r}", D) for r in range(2)]
        lhs_hi = [sb(f"lhs_hi{r}", D, F32R) for r in range(2)]
        lhs_lo = [sb(f"lhs_lo{r}", D, F32R) for r in range(2)]
        neg_part = [sb(f"neg_part{r}", REP * 2) for r in range(2)]
        neg_max = sb("neg_max", REP)
        max_parts = [sb(f"max_parts{r}", REP * 2, F32R) for r in range(4)]
        inv_sum = [sb(f"inv_sum{r}", REP) for r in range(2)]

        with ExitStack() as scope_c:
            sb = in_scope(scope_c)
            q_nat = sb("q_nat", KV_HEADS * TILES * P)
            wo_hi = sb("wo_hi", DC * D, F32R)
            wo_lo = sb("wo_lo", DC * D, F32R)
            attn = [sb(f"attn{r}", D) for r in range(2)]
            with ExitStack() as scope_ab:
                sb = in_scope(scope_ab)
                v_parts = sb("v_parts", KV_HEADS * TILES * VW, F32R)
                k_stack = sb("k_stack", KV_HEADS * TILES * P, F32R)
                with ExitStack() as scope_a:
                    sb = in_scope(scope_a)
                    W = D + 2 * KV
                    w_hi = sb("w_hi", DC * W, F32R)
                    w_lo = sb("w_lo", DC * W, F32R)
                    rope = sb("rope", TILES * 4 * HD)
                    qk_raw = [sb(f"qk_raw{r}", D + KV) for r in range(2)]
                    by_cos = [sb(f"by_cos{r}", D + KV) for r in range(2)]
                    by_sin = [sb(f"by_sin{r}", D + KV) for r in range(2)]
                    k_nat = [sb(f"k_nat{r}", KV) for r in range(2)]
                    k_parts = [sb(f"k_parts{r}", 4 * KV, F32R) for r in range(2)]
                sb = in_scope(scope_ab)
                k_blocks = sb("k_blocks", T, F32R)
                v_blocks = sb("v_blocks", QT_TILES * VW, F32R)
                probs = [sb(f"probs{r}", BANK) for r in range(4)]
                probs_hi = [sb(f"probs_hi{r}", BANK, F32R) for r in range(4)]
                probs_lo = [sb(f"probs_lo{r}", BANK, F32R) for r in range(4)]
                out_t = [sb(f"out_t{r}", BANK) for r in range(2)]
                part_hi = [sb(f"part_hi{r}", P) for r in range(2)]
                part_lo = [sb(f"part_lo{r}", P) for r in range(2)]
                q_parts = [sb(f"q_parts{r}", REP * 4 * HD, F32R) for r in range(4)]
                q_stack = [sb(f"q_stack{r}", REP * P, F32R) for r in range(QT_TILES)]
            with ExitStack() as scope_d:
                sb = in_scope(scope_d)
                xt_hi = sb("xt_hi", DC * B * T, F32R)
                xt_lo = sb("xt_lo", DC * B * T, F32R)
                wg_hi, wg_lo = [None, None], [None, None]
                wg_hi[0] = sb("wg_hi0", 6 * WORDS, F32R)
                wg_lo[0] = sb("wg_lo0", 6 * WORDS, F32R)
                codes = sb("codes", 3 * WORDS, I32)
                scales = sb("scales", 3 * WORDS)
                bits_a = sb("bits_a", WORDS, U32)
                bits_b = sb("bits_b", WORDS, U32)
                w_full = sb("w_full", 2 * WORDS)
        sb = in_scope(ctx)
        wg_hi[1] = sb("wg_hi1", 6 * WORDS, F32R)
        wg_lo[1] = sb("wg_lo1", 6 * WORDS, F32R)
        act_hi = [sb(f"act_hi{r}", BANK, F32R) for r in range(4)]
        act_lo = [sb(f"act_lo{r}", BANK, F32R) for r in range(4)]
        y_buf = [sb(f"y_buf{r}", BANK) for r in range(2)]

        psum = ctx.enter_context(nc.psum_tensor("psum", [P, 8 * BANK], F32))

        def bank(n, cols=BANK, at=0):
            return psum[:, n * BANK + at:n * BANK + at + cols]

        x_in_dma = [sem("x_in_dma0"), sem("x_in_dma1")]
        w_dma, rope_dma, wo_dma = sem("w_dma"), sem("rope_dma"), sem("wo_dma")
        consts = sem("consts")
        w_hi_done, w_lo_done = sem("w_hi_done"), sem("w_lo_done")
        wo_hi_done, wo_lo_done = sem("wo_hi_done"), sem("wo_lo_done")
        a_stats, a_mean, a_veps, a_rstd, a_xn = (sem("a_" + n) for n in ("stats", "mean", "veps", "rstd", "xn"))
        a_xt_ps, a_xt_hi, a_xt_lo = sem("a_xt_ps"), sem("a_xt_hi"), sem("a_xt_lo")
        a_qkv_ps, a_qkv_sb, a_rope, a_rotated, a_k_hi, a_k_parts, a_kt_ps, a_kt_sb = (sem("a_" + n) for n in (
            "qkv_ps", "qkv_sb", "rope", "rotated", "k_hi", "k_parts", "kt_ps", "kt_sb"))
        b_q_hi, b_q_parts, b_qt_ps, b_qt_sb = sem("b_q_hi"), sem("b_q_parts"), sem("b_qt_ps"), sem("b_qt_sb")
        b_by_query, b_part_max, b_max, b_max_hi, b_max_parts, b_mt_ps, b_mt_sb = (sem("b_" + n) for n in (
            "by_query", "part_max", "max", "max_hi", "max_parts", "mt_ps", "mt_sb"))
        b_by_key, b_exp, b_pv = sem("b_by_key"), sem("b_exp"), sem("b_pv")
        b_hi = [sem("b_hi_even"), sem("b_hi_odd")]
        b_lo = [sem("b_lo_even"), sem("b_lo_odd")]
        b_k_dma, b_v_dma = ([sem(f"b_{n}_dma{group}") for group in range(3)] for n in "kv")
        b_out_sb, b_out_ps, b_inv, b_scaled, b_out = (sem("b_" + n) for n in (
            "out_sb", "out_ps", "inv", "scaled", "out"))
        c_attn, c_at_ps, c_at_hi, c_at_lo, c_proj, c_x, c_stats, c_mean, c_veps, c_rstd, c_xn, c_xt_ps, c_xt_hi, \
            c_xt_lo = (sem("c_" + n) for n in ("attn", "at_ps", "at_hi", "at_lo", "proj", "x", "stats", "mean",
                                               "veps", "rstd", "xn", "xt_ps", "xt_hi", "xt_lo"))
        codes_dma, scales_dma = sem("codes_dma"), sem("scales_dma")
        d_bits, d_w, d_w_hi, d_w_lo = sem("d_bits"), sem("d_w"), sem("d_w_hi"), sem("d_w_lo")
        d_gate, d_up, d_square, d_inner, d_tanh, d_gelu, d_y, d_y_hi, d_y_lo, d_down, d_acc = (
            sem("d_" + n) for n in ("gate", "up", "square", "inner", "tanh", "gelu", "y", "y_hi", "y_lo", "down",
                                    "acc"))
        out_dma = sem("out_dma")
        waits_of_pool, waits_of_dve = sem("waits_of_pool"), sem("waits_of_dve")

        passed = {}

        def wait_apart(eng, sem, value):
            wait(eng, sem, value)
            if not isinstance(value, int):
                eng.sem_inc(passed[eng.engine])

        def f32(ap):
            return ap.bitcast(F32)

        def by_g(ap, cols):
            return ap.rearrange("p (g c) -> p g c", g=KV_HEADS, c=cols)

        w_raw = q_nat[:, 0:DC * W]
        wo_raw = [t[:] for t in (*xn, *attn)]

        A = Slots(TILES, period=4, first=6, lag=4)

        def v_part(t, part):
            return by_g(v_parts[:], TILES * VW)[:, :, bass.ds(t * VW + part * HD, HD)]

        def x_tile(t):
            return x_res[:, bass.ds(t * D, D)]

        ORDER = (0, 7, 1, 6, 2, 5, 3, 4)
        PLACE = [ORDER.index(i) for i in range(QT_TILES)]
        FIRST_CHUNK = [sum(i + 1 for i in ORDER[:place]) for place in range(QT_TILES)]
        BLOCK_GROUPS = ((0, 2), (2, 5), (5, 8))
        GROUP_OF = {first: group for group, (first, _) in enumerate(BLOCK_GROUPS)}
        PAIR_CHUNKS = QT_TILES * (QT_TILES + 1) // 2
        UNITS = KV_HEADS * B * QT_TILES
        BS = Slots(KV_HEADS * B * PAIR_CHUNKS, period=PAIR_CHUNKS, first=9, lag=9, lead=27)
        LEAD_PARTS, LEAD_QUERIES, LEAD_BY_QUERY, LEAD_MAXIMA = 27, 21, 15, 5

        def chunk(k, j):
            c = j % PAIR_CHUNKS
            place = max(n for n in range(QT_TILES) if FIRST_CHUNK[n] <= c)
            pair = k + j // PAIR_CHUNKS
            return pair, ORDER[place], c - FIRST_CHUNK[place], QT_TILES * pair + place, PAIR_CHUNKS * k + j

        def unit_at(k, j):
            if not BS.live(k, j):
                return None
            pair, i, kb, u, _ = chunk(k, j)
            return (pair, i, u) if kb == 0 else None

        def units_before(k, j):
            if isinstance(k, int):
                j = min(j, PAIR_CHUNKS * (UNITS // QT_TILES - k))
                if PAIR_CHUNKS * k + j <= 0:
                    return 0
            return chunk(k, j - 1)[3] + 1

        def n_parts(i):
            return -(-(i + 1) * P // BANK)

        def pieces_of(i):
            out = []
            for c in range(n_parts(i)):
                keys = min((i + 1) * P - c * BANK, BANK)
                heads = min(REP, BANK // keys)
                out += [(range(h, h + heads), c, c * BANK, keys) for h in range(0, REP, heads)]
            return out

        PIECES_BEFORE = [sum(len(pieces_of(i)) for i in ORDER[:place]) for place in range(QT_TILES + 1)]

        def wo_part(k, j):
            return j + 8 if isinstance(k, int) and k == 0 and -8 <= j < DC - 8 else None

        def pieces_at(k, j):
            if not BS.live(k, j):
                return None, [], False
            pair, i, kb, u, _ = chunk(k, j)
            p = [(PIECES_BEFORE[-1] * pair + n, n % 2, *rest) for n, rest in enumerate(
                pieces_of(i), PIECES_BEFORE[PLACE[i]])]
            return (pair, i, u), p[len(p) * kb // (i + 1):len(p) * (kb + 1) // (i + 1)], kb == i

        C = Slots(TILES, period=4, first=5, lag=4)

        def first_piece(k, j):
            return {3: 0, 13: 1, 17: 2}.get(C.period * k + j) if isinstance(k, int) else None

        GROUP_ITEMS = CHUNKS * 2
        DS = Slots(GROUPS * GROUP_ITEMS, period=2 * GROUP_ITEMS, first=GROUP_ITEMS, lag=2)
        PIECE_AT = {2: 0, 4: 1, 6: 2}

        def piece(k, j):
            if j % GROUP_ITEMS in PIECE_AT and DS.live(k, j + GROUP_ITEMS):
                m = PIECE_AT[j % GROUP_ITEMS]
                g = j // GROUP_ITEMS + 1
                return m, g % 2, 6 * k + 3 * g + m
            return None

        def columns(buf, m):
            return buf[:, m * 2 * WORDS:(m + 1) * 2 * WORDS]

        CONSTS_A = 15

        def half_count(k, j):
            return PAIR_CHUNKS // 2 * k + j // 2 + 1

        block = ctx.enter_context(nc.Block())

        @block.sync
        def _(sp):
            for u in range(TILES // 2):
                wait(sp, x_in_dma[u % 2], 16 * (u // 2))
                sp.dma_start(x_res[:, u * 2 * D:(u + 1) * 2 * D].rearrange("p (n d) -> p n d", n=2),
                             x_in[u * 2 * P:(u + 1) * 2 * P, :].rearrange("(n p) d -> p n d", p=P)
                             ).then_inc(x_in_dma[u % 2], 16)
            sp.wait_ge(a_kt_sb, TILES)
            sp.wait_ge(a_k_parts, TILES)
            sp.wait_ge(a_rope, TILES)

            for c in range(DC):
                sp.dma_start(wo_raw[c], wo_in[c * P:(c + 1) * P, :]).then_inc(wo_dma, 16)
            sp.wait_ge(b_out, KV_HEADS * TILES)
            sp.wait_ge(wo_lo_done, DC)

            def load_group(g):
                sp.dma_start(codes[:], codes_in[bass.ds(g, 1), :, :].rearrange("g p w -> (g p) w")
                             ).then_inc(codes_dma, 16)
                sp.dma_start(scales[:], scales_in[bass.ds(g, 1), :, :].rearrange("g s w -> (g s) w").unsqueeze(1)
                             .broadcast_to([P // 16, 16, 3 * WORDS])).then_inc(scales_dma, 16)

            load_group(0)
            with sp.Fori(1, GROUPS) as g:
                sp.wait_ge(d_w, g * 3)
                load_group(g)
            for j in range(CHUNKS):
                sp.wait_ge(d_acc, 4 * ((GROUPS - 1) * CHUNKS + j + 1))
                sp.dma_start(out[j * BANK:(j + 1) * BANK, :].rearrange("(n p) d -> p n d", p=P),
                             x_res[:, j * 4 * D:(j + 1) * 4 * D].rearrange("p (n d) -> p n d", n=4)
                             ).then_inc(out_dma, 16)
            sp.wait_ge(out_dma, 16 * CHUNKS)

        @block.gpsimd
        def _(pool):
            passed[pool.engine] = waits_of_pool
            pool.memset(minus_half[:], -0.5).then_inc(consts, 1)
            pool.memset(ident[:], 0.0).then_inc(consts, 1)
            pool.memset(ident_bf[:], 0.0).then_inc(consts, 1)
            pool.memset(causal[:], 0.0).then_inc(consts, 1)
            pool.memset(causal_t[:], 0.0).then_inc(consts, 1)
            for r in range(2):
                first = by_g(k_parts[r][:], P)[:, :, 0:HD]
                pool.memset(f32(first), 0.0).then_inc(consts, 1)
            pool.wait_ge(consts, 7)
            for r in range(2):
                pool.memset(f32(by_g(k_parts[r][:], P)[:, :, 0:2]), 1.0).then_inc(consts, 1)
            v_ones = v_parts[:].rearrange("p (b c) -> p b c", c=VW)[:, :, VW - 1:VW]
            pool.memset(f32(v_ones), 1.0).then_inc(consts, 1)
            for m in (ident[:], ident_bf[:]):
                pool.affine_select(out=m, in_=m, compare_op=ALU.not_equal, fill=1.0, base=0,
                                   pattern=[[-1, P]], channel_multiplier=1).then_inc(consts, 1)
            pool.affine_select(out=causal[:], in_=causal[:], compare_op=ALU.is_ge, fill=MASKED, base=0,
                               pattern=[[-1, P]], channel_multiplier=1).then_inc(consts, 1)
            causal_t3 = causal_t[:].rearrange("p (h q) -> p h q", h=REP)
            pool.affine_select(out=causal_t3, in_=causal_t3, compare_op=ALU.is_ge, fill=MASKED, base=0,
                               pattern=[[0, REP], [1, P]], channel_multiplier=-1).then_inc(consts, 1)

            pool.wait_ge(consts, CONSTS_A - 1)
            pool.tensor_copy(ident_r[:], ident[:]).then_inc(consts, 1)

            def inverse_deviation(t, r, mean_sem, veps_sem, rstd_sem):
                wait_apart(pool, mean_sem, t + 1)
                pool.tensor_scalar(var_eps[:, r:r + 1], mean_var[:, 2 * r + 1:2 * r + 2], EPS, None,
                                   ALU.add).then_inc(veps_sem, 1)
                pool.wait_ge(veps_sem, t + 1)
                pool.tensor_tensor(rstd[:, r:r + 1], var_eps[:, r:r + 1], minus_half[:],
                                   ALU.pow).then_inc(rstd_sem, 1)

            def slot_a(k, j):
                t, r = A.period * k + j, j % 4
                if A.live(k, j):
                    inverse_deviation(t, r, a_mean, a_veps, a_rstd)
                if A.live(k, j - 3):
                    t, r = t - 3, (j - 3) % 2
                    wait_apart(pool, a_rope, t + 1)
                    wait_apart(pool, a_k_parts, t - 1)
                    cos, sin = (s[r][:].rearrange("p (h a d) -> p h a d", a=2, d=HD // 2) for s in (by_cos, by_sin))
                    q_out = q_nat[:].rearrange("p (g c) -> p g c", g=KV_HEADS)[:, :, bass.ds(t * P, P)]
                    k_out = k_nat[r][:].rearrange("p (h a d) -> p h a d", a=2, d=HD // 2)
                    for a in range(2):
                        pool.tensor_tensor(
                            q_out.rearrange("p g (h a d) -> p g h a d", a=2, d=HD // 2)[:, :, :, a, :],
                            cos[:, 0:HEADS, a, :].rearrange("p (g h) d -> p g h d", g=KV_HEADS),
                            sin[:, 0:HEADS, 1 - a, :].rearrange("p (g h) d -> p g h d", g=KV_HEADS), ALU.add)
                        rot = pool.tensor_tensor(k_out[:, :, a, :], cos[:, HEADS:, a, :], sin[:, HEADS:, 1 - a, :],
                                                 ALU.add)
                    rot.then_inc(a_rotated, 1)
                    wait_apart(pool, a_rotated, t + 1)
                    wait_apart(pool, a_kt_ps, t - 1)
                    slots = k_parts[r][:].rearrange("p (g s d) -> p g s d", g=KV_HEADS, s=4)
                    k_in = k_nat[r][:].rearrange("p (g d) -> p g d", d=HD)
                    twice = k_nat[r][:].rearrange("p (g d) -> p g d", d=HD).unsqueeze(2).broadcast_to(
                        [P, KV_HEADS, 2, HD])
                    pool.tensor_copy(slots[:, :, 1:3, :], twice).then_inc(a_k_hi, 1)
                    pool.wait_ge(a_k_hi, t + 1)
                    pool.tensor_tensor(slots[:, :, 3, :], k_in, f32(slots[:, :, 1, :]),
                                       ALU.subtract).then_inc(a_k_parts, 1)

            A.run(pool, slot_a)

            pool.wait_ge(a_kt_sb, TILES)
            for r in range(4):
                pool.memset(f32(q_parts[r][:].rearrange("p (h c) -> p h c", h=REP)[:, :, 0:HD]),
                            0.0).then_inc(consts, 1)
            pool.wait_ge(consts, CONSTS_A + 4)

            def query_parts(pair, i, u):
                wait_apart(pool, b_qt_ps, u - 3)
                slots = q_parts[PLACE[i] % 4][:].rearrange("p (h s d) -> p h s d", h=REP, s=4)
                q_in = q_nat[:, bass.ds((QT_TILES * pair + i) * P, P)].rearrange("p (h d) -> p h d", h=REP)
                pool.tensor_copy(slots[:, :, 1::2, :], q_in.unsqueeze(2).broadcast_to([P, REP, 2, HD])
                                 ).then_inc(b_q_hi, 1)
                wait_apart(pool, b_q_hi, u + 1)
                pool.tensor_tensor(slots[:, :, 2, :], q_in, f32(slots[:, :, 1, :]),
                                   ALU.subtract).then_inc(b_q_parts, 1)

            def load_blocks(pair, dst, src, cols, group, done):
                first, end = BLOCK_GROUPS[group]
                pool.dma_start(dst[:, first * cols:end * cols],
                               src[:, bass.ds((QT_TILES * pair + first) * cols, (end - first) * cols)]
                               ).then_inc(done[group], 16)

            pool.wait_ge(a_rope, TILES)

            def reload(k, j, lag, used, dst, src, cols, done):
                if not (BS.live(k, j - lag) and BS.live(k, j - lag + PAIR_CHUNKS)):
                    return
                pair, i, kb, u, n = chunk(k, j - lag)
                for group, (first, end) in enumerate(BLOCK_GROUPS):
                    last_user = [tile for tile in ORDER if tile >= first][-1]
                    if (i, kb) == (last_user, min(last_user, end - 1)):
                        pool.wait_ge(used, n + 1)
                        load_blocks(pair + 1, dst, src, cols, group, done)

            def slot_b(k, j):
                if unit := unit_at(k, j + LEAD_PARTS):
                    query_parts(*unit)
                if BS.live(k, j - 1) and j % 2 == 1:
                    r = (j - 1) % 4
                    n = PAIR_CHUNKS * k + j - 1
                    pool.wait_ge(b_hi[0], half_count(k, j - 1))
                    pool.tensor_tensor(probs_lo[r][:], probs[r][:], f32(probs_hi[r][:]),
                                       ALU.subtract).then_inc(b_lo[0], 1)
                if isinstance(k, int) and k == 0 and -15 <= j < -12:
                    load_blocks(0, k_blocks, k_stack, P, j + 15, b_k_dma)
                    load_blocks(0, v_blocks, v_parts, VW, j + 15, b_v_dma)
                reload(k, j, 1, b_by_key, k_blocks, k_stack, P, b_k_dma)
                reload(k, j, 4, b_pv, v_blocks, v_parts, VW, b_v_dma)
                if BS.live(k, j - 9):
                    pair, i, kb, u, n = chunk(k, j - 9)
                    if kb == i:
                        wait_apart(pool, b_scaled, u + 1)
                        r = PLACE[i] % 2
                        pool.tensor_tensor(q_nat[:, bass.ds((QT_TILES * pair + i) * P, P)], part_hi[r][:], part_lo[r][:],
                                           ALU.add).then_inc(b_out, 1)

            BS.run(pool, slot_b)
            pool.wait_ge(b_out, KV_HEADS * TILES)

            def weights_low(m, buf, n):
                pool.wait_ge(d_w_hi, n + 1)
                pool.tensor_tensor(columns(wg_lo[buf], m), w_full[:], f32(columns(wg_hi[buf], m)),
                                   ALU.subtract).then_inc(d_w_lo, 1)

            def slot_c(k, j):
                t = C.period * k + j
                if C.live(k, j - 2):
                    inverse_deviation(t - 2, j % 2, c_mean, c_veps, c_rstd)
                if (m := first_piece(k, j - 1)) is not None:
                    weights_low(m, 0, m)

            C.run(pool, slot_c)

            def slot_d(k, j):
                s = DS.period * k + j
                if p := piece(k, j):
                    weights_low(*p)
                if DS.live(k, j):
                    pool.wait_ge(d_y_hi, s + 1)
                    pool.tensor_tensor(act_lo[j % 4][:], y_buf[j % 2][:], f32(act_hi[j % 4][:]),
                                       ALU.subtract).then_inc(d_y_lo, 1)

            DS.run(pool, slot_d)

        @block.scalar
        def _(act):
            w3 = w_raw.rearrange("p (c n) -> p c n", c=DC)
            for src, at, n in ((wq_in, 0, D), (wk_in, D, KV), (wv_in, D + KV, KV)):
                act.dma_start(w3[:, :, at:at + n], src.rearrange("(c p) n -> p c n", p=P)).then_inc(w_dma, 16)
            for b in range(B):
                act.dma_start(rope[:].rearrange("p (b n c) -> p b n c", b=B, n=QT_TILES)[:, b],
                              rope_in.rearrange("(n p) c -> p n c", p=P)).then_inc(rope_dma, 16)
            act.wait_ge(w_dma, 48)
            act.activation(w_hi[:], w_raw, ACT.Copy).then_inc(w_hi_done, 1)

            def slot_a(k, j):
                t = A.period * k + j
                if A.live(k, j - 1):
                    r = (j - 1) % 2
                    act.wait_ge(a_xt_ps, t)
                    wait(act, a_qkv_ps, t - 2)
                    act.activation(lhs_hi[r][:], bank(r), ACT.Copy).then_inc(a_xt_hi, 1)
                if A.live(k, j - 4):
                    act.wait_ge(a_kt_ps, t - 3)
                    act.activation(by_g(k_stack[:], B * T)[:, :, bass.ds((t - 4) * P, P)],
                                   by_g(bank(6 + j % 2), P), ACT.Copy).then_inc(a_kt_sb, 1)
                if A.live(k, j - 2):
                    r = j % 2
                    act.wait_ge(a_qkv_ps, t - 1)
                    wait(act, a_rope, t - 3)
                    act.activation(v_part(t - 2, 0),
                                   by_g(bank(3 + 2 * r, KV, KV), HD), ACT.Copy)
                    act.activation(qk_raw[r][:], psum[:, (2 + 2 * r) * BANK:(2 + 2 * r) * BANK + D + KV],
                                   ACT.Copy).then_inc(a_qkv_sb, 1)

            A.run(act, slot_a)

            def queries_out(pair, i, u):
                act.wait_ge(b_qt_ps, u + 1)
                act.activation(q_stack[i][:], bank(5), ACT.Copy).then_inc(b_qt_sb, 1)

            def maxima_out(pair, i, u):
                act.wait_ge(b_mt_ps, u + 1)
                act.activation(q_stack[i][0:2, :], psum[0:2, 5 * BANK:6 * BANK], ACT.Copy).then_inc(b_mt_sb, 1)

            def slot_b(k, j):
                if (c := wo_part(k, j)) is not None:
                    act.wait_ge(wo_dma, 16 * DC)
                    act.activation(wo_hi[:, c * D:(c + 1) * D], wo_raw[c], ACT.Copy).then_inc(wo_hi_done, 1)
                if BS.live(k, j):
                    pair, i, kb, u, n = chunk(k, j)
                    act.wait_ge(b_by_key, n + 1)
                    wait(act, b_pv, n - 3)
                    act.activation(probs[j % 4][:], bank(2 + j % 2), ACT.Exp).then_inc(b_exp, 1)
                if unit := unit_at(k, j + LEAD_MAXIMA):
                    maxima_out(*unit)
                if unit := unit_at(k, j + LEAD_QUERIES):
                    queries_out(*unit)
                if BS.live(k, j) and j % 2 == 0:
                    act.wait_ge(b_exp, PAIR_CHUNKS * k + j + 1)
                    act.activation(probs_hi[j % 4][:], probs[j % 4][:], ACT.Copy).then_inc(b_hi[0], 1)
                if BS.live(k, j - 4):
                    pair, i, kb, u, n = chunk(k, j - 4)
                    if kb == i:
                        act.wait_ge(b_pv, n + 1)
                        wait(act, b_out_ps, u - 1)
                        act.activation(out_t[PLACE[i] % 2][0:VW, :], bank(4 + 3 * (PLACE[i] % 2))[0:VW, :],
                                       ACT.Copy).then_inc(b_out_sb, 1)

            BS.run(act, slot_b)
            act.wait_ge(b_out, KV_HEADS * TILES - QT_TILES)

            def weights_high(m, buf, n):
                act.wait_ge(d_w, n + 1)
                act.activation(columns(wg_hi[buf], m), w_full[:], ACT.Copy).then_inc(d_w_hi, 1)

            def slot_c(k, j):
                t = C.period * k + j
                if C.live(k, j):
                    wait(act, c_at_ps, t - 1)
                    act.activation(by_g(attn[j % 2][:], P), by_g(q_nat[:], TILES * P)[:, :, bass.ds(t * P, P)],
                                   ACT.Copy).then_inc(c_attn, 1)
                if C.live(k, j - 1):
                    r = (j - 1) % 2
                    act.wait_ge(c_at_ps, t)
                    wait(act, c_proj, t - 2)
                    act.activation(lhs_hi[r][:], bank(r), ACT.Copy).then_inc(c_at_hi, 1)
                if C.live(k, j - 4):
                    if isinstance(k, int) and t == 4:
                        act.wait_ge(b_out, KV_HEADS * TILES)
                    act.wait_ge(c_xt_ps, t - 3)
                    act.activation(xt_hi[:].rearrange("p (c t) -> p c t", c=DC)[:, :, bass.ds((t - 4) * P, P)],
                                   bank(4 + j % 2).rearrange("p (c t) -> p c t", c=DC),
                                   ACT.Copy).then_inc(c_xt_hi, 1)
                if (m := first_piece(k, j - 1)) is not None:
                    weights_high(m, 0, m)

            C.run(act, slot_c)

            def slot_d(k, j):
                s = DS.period * k + j
                if DS.live(k, j):
                    y = y_buf[j % 2]
                    act.wait_ge(d_gate, s + 1)
                    wait(act, d_y_lo, s - 1)
                    act.activation(y[:], bank(j % 2), ACT.Square).then_inc(d_square, 1)
                    act.wait_ge(d_inner, s + 1)
                    act.activation(y[:], y[:], ACT.Tanh, scale=GELU_C * GELU_A).then_inc(d_tanh, 1)
                if p := piece(k, j):
                    wait(act, d_down, DS.period * k + j // GROUP_ITEMS * GROUP_ITEMS)
                    weights_high(*p)
                if DS.live(k, j):
                    act.wait_ge(d_y, s + 1)
                    wait(act, d_down, s - 3)
                    act.activation(act_hi[j % 4][:], y[:], ACT.Copy).then_inc(d_y_hi, 1)

            DS.run(act, slot_d)

        @block.vector
        def _(dve):
            passed[dve.engine] = waits_of_dve
            def moments(t, r, r4, stats_sem, mean_sem):
                st = stats[:, 6 * r:6 * r + 6]
                dve.bn_stats(st, x_tile(t)).then_inc(stats_sem, 1)
                wait_apart(dve, stats_sem, t + 1)
                dve.bn_aggr(mean_var[:, 2 * r4:2 * r4 + 2], st).then_inc(mean_sem, 1)

            def normalise(t, r, r4, xn_sem):
                dve.tensor_scalar(xn[r][:], x_tile(t), mean_var[:, 2 * r4:2 * r4 + 1], rstd[:, r4:r4 + 1],
                                  ALU.subtract, ALU.mult).then_inc(xn_sem, 1)

            def slot_a(k, j):
                t = A.period * k + j
                if A.live(k, j):
                    wait_apart(dve, x_in_dma[j // 2 % 2], 16 * (k + j // 4 + 1))
                    moments(t, j % 2, j % 4, a_stats, a_mean)
                if A.live(k, j - 1):
                    dve.wait_ge(a_rstd, t)
                    wait(dve, a_xt_ps, t - 2)
                    normalise(t - 1, (j - 1) % 2, (j - 1) % 4, a_xn)
                if j == 1 and isinstance(k, int) and k == 0:
                    dve.wait_ge(w_hi_done, 1)
                    dve.tensor_tensor(w_lo[:], w_raw, f32(w_hi[:]), ALU.subtract).then_inc(w_lo_done, 1)
                    dve.wait_ge(rope_dma, 32)
                if A.live(k, j - 3):
                    r = (j - 3) % 2
                    dve.wait_ge(a_qkv_sb, t - 2)
                    v_ps = by_g(bank(3 + 2 * r, KV, KV), HD)
                    dve.tensor_tensor(v_part(t - 3, 1), v_ps, f32(v_part(t - 3, 0)), ALU.subtract)
                    wait(dve, a_rotated, t - 4)
                    for i, (at, n) in enumerate(((0, HEADS), (D, KV_HEADS))):
                        for which, dst in enumerate((by_cos[r], by_sin[r])):
                            table = rope[:, bass.ds((t - 3) * 4 * HD + (2 * i + which) * HD, HD)]
                            last = dve.tensor_tensor(
                                dst[:, at:at + n * HD].rearrange("p (h d) -> p h d", d=HD),
                                qk_raw[r][:, at:at + n * HD].rearrange("p (h d) -> p h d", d=HD),
                                table.unsqueeze(1).broadcast_to([P, n, HD]), ALU.mult)
                    last.then_inc(a_rope, 1)
                if A.live(k, j - 1):
                    r = (j - 1) % 2
                    dve.wait_ge(a_xt_hi, t)
                    dve.tensor_tensor(lhs_lo[r][:], bank(r), f32(lhs_hi[r][:]), ALU.subtract).then_inc(a_xt_lo, 1)

            A.run(dve, slot_a)

            def row_maxima(unit, its_pieces, last):
                pair, i, u = unit
                for n, r, heads, c, at, keys in its_pieces:
                    dve.wait_ge(b_by_query, n + 1)
                    dve.tensor_reduce(
                        neg_part[PLACE[i] % 2][:].rearrange("p (h c) -> p h c", h=REP)[:, heads.start:heads.stop, c],
                        bank(r, len(heads) * keys).rearrange("p (h k) -> p h k", h=len(heads)), axis=AX_X,
                        op=ALU.max, negate=True).then_inc(b_part_max, 1)
                if last:
                    dve.wait_ge(b_part_max, its_pieces[-1][0] + 1)
                    each = neg_part[PLACE[i] % 2][:].rearrange("p (h c) -> p h c", h=REP)[:, :, 0:n_parts(i)]
                    dve.tensor_reduce(neg_max[:], each, axis=AX_X, op=ALU.min).then_inc(b_max, 1)
                    dve.wait_ge(b_max, u + 1)
                    wait(dve, b_mt_ps, u - 3)
                    both = max_parts[PLACE[i] % 4][:].rearrange("p (h s) -> p h s", h=REP)
                    dve.tensor_copy(both[:, :, 0], neg_max[:]).then_inc(b_max_hi, 1)
                    dve.wait_ge(b_max_hi, u + 1)
                    dve.tensor_tensor(both[:, :, 1], neg_max[:], f32(both[:, :, 0]),
                                      ALU.subtract).then_inc(b_max_parts, 1)

            def slot_b(k, j):
                if (c := wo_part(k, j)) is not None:
                    part = slice(c * D, (c + 1) * D)
                    dve.wait_ge(wo_hi_done, c + 1)
                    dve.tensor_tensor(wo_lo[:, part], wo_raw[c], f32(wo_hi[:, part]),
                                      ALU.subtract).then_inc(wo_lo_done, 1)
                unit, its_pieces, last = pieces_at(k, j + LEAD_BY_QUERY)
                if unit:
                    row_maxima(unit, its_pieces, last)
                if BS.live(k, j - 1) and j % 2 == 0:
                    r = (j - 1) % 4
                    dve.wait_ge(b_exp, PAIR_CHUNKS * k + j)
                    dve.tensor_copy(probs_hi[r][:], probs[r][:]).then_inc(b_hi[1], 1)
                    dve.wait_ge(b_hi[1], half_count(k, j - 1))
                    dve.tensor_tensor(probs_lo[r][:], probs[r][:], f32(probs_hi[r][:]),
                                      ALU.subtract).then_inc(b_lo[1], 1)
                if BS.live(k, j - 7):
                    pair, i, kb, u, n = chunk(k, j - 7)
                    if kb == i:
                        out3 = bank(6, REP * VW).rearrange("p (h c) -> p h c", h=REP)
                        inv = inv_sum[PLACE[i] % 2]
                        dve.wait_ge(b_out_ps, u + 1)
                        dve.reciprocal(inv[:], out3[:, :, VW - 1]).then_inc(b_inv, 1)
                        dve.wait_ge(b_inv, u + 1)
                        wait(dve, b_out, u - 1)
                        inv3 = inv[:].unsqueeze(2).broadcast_to([P, REP, HD])
                        for dst, at in ((part_hi, 0), (part_lo, HD)):
                            last = dve.tensor_tensor(dst[PLACE[i] % 2][:].rearrange("p (h d) -> p h d", h=REP),
                                                     out3[:, :, at:at + HD], inv3, ALU.mult)
                        last.then_inc(b_scaled, 1)

            BS.run(dve, slot_b)

            def unpack(m, n, group_count):
                if m == 0:
                    dve.wait_ge(codes_dma, group_count)
                    dve.wait_ge(scales_dma, group_count)
                words = codes[:, m * WORDS:(m + 1) * WORDS].bitcast(U32)
                dve.tensor_scalar(bits_a[:], words, 12, 0xF0000, ALU.logical_shift_left,
                                  ALU.bitwise_and).then_inc(d_bits, 1)
                dve.wait_ge(d_bits, 4 * n + 1)
                dve.scalar_tensor_tensor(bits_b[:], words, 0xF, bits_a[:], ALU.bitwise_and,
                                         ALU.bitwise_or).then_inc(d_bits, 1)
                dve.wait_ge(d_bits, 4 * n + 2)
                dve.scalar_tensor_tensor(bits_a[:], bits_b[:], 3, bits_b[:], ALU.logical_shift_left,
                                         ALU.bitwise_or).then_inc(d_bits, 1)
                dve.wait_ge(d_bits, 4 * n + 3)
                dve.tensor_scalar(bits_b[:], bits_a[:], 1, 0x008E008E, ALU.logical_shift_left,
                                  ALU.bitwise_and).then_inc(d_bits, 1)
                wait_apart(dve, d_bits, 4 * n + 4)
                wait_apart(dve, d_w_lo, n)
                value = bits_b[:].bitcast(FP8).rearrange("p (w b) -> p b w", b=4)
                for nibble in range(2):
                    last = dve.scalar_tensor_tensor(w_full[:, nibble * WORDS:(nibble + 1) * WORDS],
                                                    value[:, 2 * nibble, :], CODE_SCALE,
                                                    scales[:, m * WORDS:(m + 1) * WORDS], ALU.mult, ALU.mult)
                last.then_inc(d_w, 1)

            def slot_c(k, j):
                t = C.period * k + j
                if C.live(k, j - 1):
                    r = (j - 1) % 2
                    dve.wait_ge(c_at_hi, t)
                    dve.tensor_tensor(lhs_lo[r][:], bank(r), f32(lhs_hi[r][:]), ALU.subtract).then_inc(c_at_lo, 1)
                if C.live(k, j - 3):
                    dve.wait_ge(c_rstd, t - 2)
                    wait(dve, c_xt_ps, t - 4)
                    normalise(t - 3, (j - 3) % 2, (j - 3) % 2, c_xn)
                if C.live(k, j - 4):
                    dve.wait_ge(c_xt_hi, t - 3)
                    dst, hi = (b[:].rearrange("p (c t) -> p c t", c=DC)[:, :, bass.ds((t - 4) * P, P)]
                               for b in (xt_lo, xt_hi))
                    dve.tensor_tensor(dst, bank(4 + j % 2).rearrange("p (c t) -> p c t", c=DC), f32(hi),
                                      ALU.subtract).then_inc(c_xt_lo, 1)
                if C.live(k, j - 2):
                    dve.wait_ge(c_proj, t - 1)
                    dve.tensor_tensor(x_tile(t - 2), x_tile(t - 2), bank(2 + j % 2), ALU.add).then_inc(c_x, 1)
                    wait_apart(dve, c_x, t - 1)
                    moments(t - 2, j % 2, j % 2, c_stats, c_mean)
                if (m := first_piece(k, j)) is not None:
                    unpack(m, m, 16)

            C.run(dve, slot_c)

            def slot_d(k, j):
                s = DS.period * k + j
                y, gate, up = y_buf[j % 2], bank(j % 2), bank(2 + j % 2)
                if DS.live(k, j):
                    dve.wait_ge(d_square, s + 1)
                    dve.scalar_tensor_tensor(y[:], y[:], 1.0 / GELU_A, gate, ALU.add, ALU.mult).then_inc(d_inner, 1)
                if p := piece(k, j):
                    m, buf, n = p
                    unpack(m, n, 16 * (2 * k + j // GROUP_ITEMS + 2))
                if DS.live(k, j):
                    dve.wait_ge(d_tanh, s + 1)
                    dve.scalar_tensor_tensor(y[:], y[:], 1.0, gate, ALU.add, ALU.mult).then_inc(d_gelu, 1)
                    dve.wait_ge(d_gelu, s + 1)
                    dve.wait_ge(d_up, s + 1)
                    dve.scalar_tensor_tensor(y[:], y[:], 0.5, up, ALU.mult, ALU.mult).then_inc(d_y, 1)
                if j % 2 == 1 and DS.live(k, j - 2):
                    dve.wait_ge(d_down, s - 1)
                    for n in range(4):
                        tile = (j - 2) // 2 % CHUNKS * 4 + n
                        x = x_res[:, tile * D:(tile + 1) * D]
                        dve.tensor_tensor(x, x, bank(4 + n), ALU.add).then_inc(d_acc, 1)

            DS.run(dve, slot_d)

        @block.tensor
        def _(pe):
            pe.wait_ge(consts, CONSTS_A)

            def split_product(dst, lhs, rhs, first=True, last=True, n=DC):
                for c in range(n):
                    for q, (a, b) in enumerate(((0, 0), (0, 1), (1, 0))):
                        mm = pe.matmul(dst, lhs(a, c), rhs(b, c), start=first and c == 0 and q == 0,
                                       stop=last and c == n - 1 and q == 2)
                return mm

            def slot_a(k, j):
                t = A.period * k + j
                if A.live(k, j - 1):
                    r = (j - 1) % 2
                    pe.wait_ge(a_xn, t)
                    wait(pe, a_xt_lo, t - 2)
                    for c in range(DC):
                        tr = pe.transpose(bank(r, P, c * P), xn[r][:, c * P:(c + 1) * P], ident[:])
                    tr.then_inc(a_xt_ps, 1)
                if A.live(k, j - 2):
                    r = j % 2
                    if isinstance(k, int) and t == 2:
                        pe.wait_ge(w_lo_done, 1)
                    pe.wait_ge(a_xt_hi, t - 1)
                    pe.wait_ge(a_xt_lo, t - 1)
                    wait(pe, a_qkv_sb, t - 3)
                    wait(pe, a_rope, t - 3)
                    for dst, at, n in ((bank(2 + 2 * r), 0, D), (bank(3 + 2 * r, 2 * KV), D, 2 * KV)):
                        mm = split_product(
                            dst, lambda a, c: (lhs_hi, lhs_lo)[a][r][:, c * P:(c + 1) * P],
                            lambda b, c: (w_hi, w_lo)[b][:, c * W + at:c * W + at + n])
                    mm.then_inc(a_qkv_ps, 1)
                if A.live(k, j - 4):
                    r = j % 2
                    pe.wait_ge(a_k_parts, t - 3)
                    wait(pe, a_kt_sb, t - 5)
                    for g in range(KV_HEADS):
                        tr = pe.transpose(bank(6 + r, P, g * P), f32(k_parts[r][:, g * P:(g + 1) * P]), ident[:])
                    tr.then_inc(a_kt_ps, 1)

            A.run(pe, slot_a)
            pe.wait_ge(a_kt_sb, TILES)

            def queries(pair, i, u, maxima_before):
                pe.wait_ge(b_q_parts, u + 1)
                wait(pe, b_qt_sb, u)
                wait(pe, b_mt_sb, maxima_before)
                for h in range(REP):
                    tr = pe.transpose(bank(5, P, h * P), f32(q_parts[PLACE[i] % 4][:, h * P:(h + 1) * P]), ident[:])
                tr.then_inc(b_qt_ps, 1)

            def maxima(pair, i, u, queries_before):
                pe.wait_ge(b_max_parts, u + 1)
                wait(pe, b_qt_sb, queries_before)
                wait(pe, b_mt_sb, u)
                for h in range(REP):
                    tr = pe.matmul(psum[0:2, 5 * BANK + h * P:5 * BANK + (h + 1) * P],
                                   max_parts[PLACE[i] % 4][:, 2 * h:2 * h + 2], ident_r[:], start=True, stop=True)
                tr.then_inc(b_mt_ps, 1)

            def scores_by_query(unit, its_pieces):
                pair, i, u = unit
                for n, r, heads, c, at, keys in its_pieces:
                    pe.wait_ge(b_qt_sb, u + 1)
                    wait(pe, b_part_max, n - 1)
                    diagonal = at + keys == (i + 1) * P
                    for place, h in enumerate(heads):
                        mm = pe.matmul(bank(r, keys, place * keys), q_stack[i][:, h * P:(h + 1) * P],
                                       k_stack[:, bass.ds(pair * T + at, keys)], start=True, stop=not diagonal)
                        if diagonal:
                            mm = pe.matmul(bank(r, P, (place + 1) * keys - P), ident_bf[:], causal[:],
                                           start=False, stop=True)
                    mm.then_inc(b_by_query, 1)

            def slot_b(k, j):
                if BS.live(k, j):
                    pair, i, kb, u, n = chunk(k, j)
                    if kb == 0:
                        pe.wait_ge(b_mt_sb, u + 1)
                    if kb in GROUP_OF and PLACE[i] < 2:
                        pe.wait_ge(b_k_dma[GROUP_OF[kb]], 16 * (pair + 1))
                    wait(pe, b_exp, n - 1)
                    mm = pe.matmul(bank(2 + j % 2), k_blocks[:, kb * P:(kb + 1) * P], q_stack[i][:],
                                   start=True, stop=kb != i)
                    if kb == i:
                        mm = pe.matmul(bank(2 + j % 2), ident_bf[:], causal_t[:], start=False, stop=True)
                    mm.then_inc(b_by_key, 1)
                unit, its_pieces, _ = pieces_at(k, j + LEAD_BY_QUERY)
                if unit:
                    scores_by_query(unit, its_pieces)
                if unit := unit_at(k, j + LEAD_MAXIMA):
                    maxima(*unit, units_before(k, j + LEAD_QUERIES))
                if unit := unit_at(k, j + LEAD_QUERIES):
                    queries(*unit, units_before(k, j + LEAD_MAXIMA + 1))
                if BS.live(k, j - 3):
                    pair, i, kb, u, n = chunk(k, j - 3)
                    if kb == 0:
                        wait(pe, b_out_sb, u - 1)
                    if kb in GROUP_OF and PLACE[i] < 2:
                        pe.wait_ge(b_v_dma[GROUP_OF[kb]], 16 * (pair + 1))
                    r = (j - 3) % 4
                    pe.wait_ge(b_lo[r % 2], half_count(k, j - 3))
                    for q, part in enumerate((probs_hi, probs_lo)):
                        mm = pe.matmul(bank(4 + 3 * (PLACE[i] % 2))[0:VW, :],
                                       v_blocks[:, kb * VW:(kb + 1) * VW], part[r][:],
                                       start=kb == 0 and q == 0, stop=kb == i and q == 1)
                    mm.then_inc(b_pv, 1)
                if BS.live(k, j - 6):
                    pair, i, kb, u, n = chunk(k, j - 6)
                    if kb == i:
                        pe.wait_ge(b_out_sb, u + 1)
                        wait(pe, b_scaled, u)
                        for h in range(REP):
                            tr = pe.transpose(bank(6, VW, h * VW), out_t[PLACE[i] % 2][0:VW, h * P:(h + 1) * P],
                                              ident[0:VW, 0:VW])
                        tr.then_inc(b_out_ps, 1)

            BS.run(pe, slot_b)
            pe.wait_ge(wo_lo_done, DC)
            pe.wait_ge(b_part_max, KV_HEADS * B * PIECES_BEFORE[-1])
            pe.wait_ge(b_exp, BS.count)
            pe.wait_ge(b_mt_sb, UNITS)
            pe.wait_ge(b_out_sb, UNITS)

            def slot_c(k, j):
                t = C.period * k + j
                if C.live(k, j - 1):
                    r = (j - 1) % 2
                    pe.wait_ge(c_attn, t)
                    wait(pe, c_at_lo, t - 2)
                    for c in range(DC):
                        tr = pe.transpose(bank(r, P, c * P), attn[r][:, c * P:(c + 1) * P], ident[:])
                    tr.then_inc(c_at_ps, 1)
                if C.live(k, j - 2):
                    r = j % 2
                    pe.wait_ge(c_at_hi, t - 1)
                    pe.wait_ge(c_at_lo, t - 1)
                    wait(pe, c_x, t - 3)
                    mm = split_product(bank(2 + r), lambda a, c: (lhs_hi, lhs_lo)[a][r][:, c * P:(c + 1) * P],
                                       lambda b, c: (wo_hi, wo_lo)[b][:, c * D:(c + 1) * D])
                    mm.then_inc(c_proj, 1)
                if C.live(k, j - 4):
                    r = j % 2
                    pe.wait_ge(c_xn, t - 3)
                    wait(pe, c_xt_lo, t - 5)
                    for c in range(DC):
                        half, parity = c // 2, c % 2
                        tr = pe.transpose(bank(4 + r, P, c * P),
                                          xn[r][:, half * 2 * P + parity:(half + 1) * 2 * P:2], ident[:])
                    tr.then_inc(c_xt_ps, 1)

            C.run(pe, slot_c)
            pe.wait_ge(c_xt_lo, TILES)

            def slot_d(k, j):
                s = DS.period * k + j
                if DS.live(k, j):
                    g, chunk, half = j // GROUP_ITEMS, j // 2 % CHUNKS, j % 2
                    wait(pe, d_y, s - 1)
                    for m, done in ((0, d_gate), (1, d_up)):
                        if j % GROUP_ITEMS == 0:
                            pe.wait_ge(d_w_lo, 6 * k + 3 * g + m + 1)
                        split_product(
                            bank(2 * m + j % 2),
                            lambda a, c: columns((wg_hi, wg_lo)[a][g % 2], m)[
                                :, c % 2 * WORDS + c // 2 * GROUP + half * P:
                                c % 2 * WORDS + c // 2 * GROUP + (half + 1) * P],
                            lambda b, c: (xt_hi, xt_lo)[b][:, c * B * T + chunk * BANK:
                                                           c * B * T + (chunk + 1) * BANK]).then_inc(done, 1)
                if DS.live(k, j - 2):
                    i = j - 2
                    g, half = i // GROUP_ITEMS, i % 2
                    if i % GROUP_ITEMS == 0:
                        pe.wait_ge(d_w_lo, 6 * k + 3 * g + 3)
                    pe.wait_ge(d_y_hi, s - 1)
                    pe.wait_ge(d_y_lo, s - 1)
                    for n in range(4):
                        if half == 0:
                            wait(pe, d_acc, 4 * (DS.period // 2 * k + i // 2 - 1) + n + 1)
                        mm = split_product(
                            bank(4 + n), lambda a, c: (act_hi, act_lo)[a][i % 4][:, n * P:(n + 1) * P],
                            lambda b, c: columns((wg_hi, wg_lo)[b][g % 2], 2)[:, half * WORDS:(half + 1) * WORDS],
                            first=half == 0, last=half == 1, n=1)
                    mm.then_inc(d_down, 1)

            DS.run(pe, slot_d)


def rope_tables():
    freqs = (1.0 / np.float32(10000.0) ** (np.arange(0, HD, 2, dtype=np.float32) / np.float32(HD))).astype(np.float32)
    angle = np.arange(T, dtype=np.float32)[:, None] * freqs[None, :]
    cos, sin = np.cos(angle), np.sin(angle)
    q = np.concatenate([cos, cos, sin, -sin], axis=1)
    return np.concatenate([q, q / np.float32(np.sqrt(HD))], axis=1).astype(np.float32)


def kernel(**inputs):
    import concourse.bacc as bacc
    from concourse.bass_utils import run_bass_kernel_spmd

    a = {n.split("_", 1)[1]: np.asarray(v) for n, v in inputs.items()}
    pair, blocks = P, GROUP // QBLOCK
    codes, scales = [], []
    for n in ("gate", "up"):
        w = a[f"ffn_{n}_W_packed"].reshape(GROUPS, pair, 2, 2, P)
        codes.append(w.transpose(0, 4, 3, 2, 1).reshape(GROUPS, P, WORDS))
        s = a[f"ffn_{n}_scales"].reshape(GROUPS, pair, 2, 2, blocks)
        scales.append(s.transpose(0, 4, 3, 2, 1).reshape(GROUPS, blocks, WORDS))
    codes.append(a["ffn_down_W_packed"].reshape(D, GROUPS, P).transpose(1, 2, 0))
    scales.append(a["ffn_down_scales"].reshape(D, GROUPS, blocks).transpose(1, 2, 0))
    arrays = {
        "x": a["attn_x"].reshape(B * T, D), "wq": a["attn_wq"], "wk": a["attn_wk"], "wv": a["attn_wv"],
        "wo": a["attn_wo"], "rope": rope_tables(),
        "codes": np.concatenate(codes, axis=2), "scales": np.concatenate(scales, axis=2),
    }
    arrays = {n: np.ascontiguousarray(v) for n, v in arrays.items()}
    nc = bacc.Bacc("TRN2", target_bir_lowering=False, num_devices=1)
    args = [nc.dram_tensor(f"in_{n}", v.shape, mybir.dt.from_np(v.dtype), kind="ExternalInput").ap()
            for n, v in arrays.items()]
    out = nc.dram_tensor("out", (B * T, D), F32, kind="ExternalOutput").ap()
    block_kernel(nc, *args, out)
    r = run_bass_kernel_spmd(nc, [{f"in_{n}": v for n, v in arrays.items()}], core_ids=[0])
    return r.results[0]["out"].reshape(B, T, D)
```
